# Optimizing a Trainium2 kernel written in Bass

```python
import numpy as np
import jax
import jax.numpy as jnp

def _softmax(x, axis=-1):
    return jax.nn.softmax(x, axis=axis)

def _gelu(x):
    return jax.nn.gelu(x, approximate=True)

def _silu(x):
    return jax.nn.silu(x)

def _sigmoid(x):
    return jax.nn.sigmoid(x)

def _layernorm(x, axis=-1, eps=1e-05):
    m = jnp.mean(x, axis=axis, keepdims=True)
    v = jnp.var(x, axis=axis, keepdims=True)
    return (x - m) / jnp.sqrt(v + eps)

def _scatter_add(tgt, idx, src, axis=0):
    return tgt.at[idx].add(src)

def _segment_sum(src, seg, n):
    return jax.ops.segment_sum(src, seg, n)
kernel_name = 'mk_adaln_d1_jaxref_r8_6bc953'

def setup_inputs(seed: int=0):
    np.random.seed(seed)
    _w = jnp.asarray

    def _L0_attn_setup():
        import jax, jax.numpy as jnp
        import numpy as np
        B, T, C = (8, 512, 128)

        def _wkv(w_decay, u_first, k, v):
            w = -jnp.exp(w_decay)
            u = u_first
            kt = jnp.transpose(k, (1, 0, 2))
            vt = jnp.transpose(v, (1, 0, 2))
            a0 = jnp.zeros((k.shape[0], k.shape[2]), dtype=k.dtype)
            b0 = jnp.zeros_like(a0)
            p0 = jnp.full_like(a0, -1e+38)

            def step(carry, kv):
                a, b, p = carry
                k_t, v_t = kv
                q = jnp.maximum(p, u + k_t)
                e1 = jnp.exp(p - q)
                e2 = jnp.exp(u + k_t - q)
                y = (e1 * a + e2 * v_t) / (e1 * b + e2)
                q2 = jnp.maximum(p + w, k_t)
                f1 = jnp.exp(p + w - q2)
                f2 = jnp.exp(k_t - q2)
                return ((f1 * a + f2 * v_t, f1 * b + f2, q2), y)
            _, y = jax.lax.scan(step, (a0, b0, p0), (kt, vt))
            return jnp.transpose(y, (1, 0, 2))
        key = jax.random.key(seed)
        ks = jax.random.split(key, 5)
        scales = (jnp.arange(C, dtype=jnp.float32) / C).reshape(1, 1, C)
        return {'x': jax.random.normal(ks[0], (B, T, C), dtype=jnp.float32), 'time_decay': scales, 'time_first': scales, 'time_mix_k': scales, 'time_mix_v': scales, 'time_mix_r': scales, 'Wk': jax.random.normal(ks[1], (C, C), dtype=jnp.float32) / np.sqrt(C), 'Wv': jax.random.normal(ks[2], (C, C), dtype=jnp.float32) / np.sqrt(C), 'Wr': jax.random.normal(ks[3], (C, C), dtype=jnp.float32) / np.sqrt(C), 'Wo': jax.random.normal(ks[4], (C, C), dtype=jnp.float32) / np.sqrt(C)}
    _L0_attn_in = _L0_attn_setup()

    def _L0_ffn_setup():
        import jax, jax.numpy as jnp
        import numpy as np
        from jax import lax
        T, B, I, M, O = (32, 64, 128, 128, 128)

        def _xavier(key, shape):
            fan_out, fan_in = shape
            limit = float(np.sqrt(6.0 / (fan_in + fan_out)))
            return jax.random.uniform(key, shape, jnp.float32, -limit, limit)
        key = jax.random.key(seed)
        ks = jax.random.split(key, 9)
        x = jax.random.normal(ks[0], (T, B, I), jnp.float32)
        return {'x': x, 'wf': _xavier(ks[1], (M, I)), 'uf': _xavier(ks[2], (M, M)), 'bf': jnp.zeros((M,), jnp.float32), 'wi': _xavier(ks[3], (M, I)), 'ui': _xavier(ks[4], (M, M)), 'bi': jnp.zeros((M,), jnp.float32), 'wc': _xavier(ks[5], (M, I)), 'uc': _xavier(ks[6], (M, M)), 'bc': jnp.zeros((M,), jnp.float32), 'wo': _xavier(ks[7], (O, I)), 'uo': _xavier(ks[8], (O, M)), 'bo': jnp.zeros((O,), jnp.float32), 'in_c': jnp.zeros((M,), jnp.float32)}
    _L0_ffn_in = _L0_ffn_setup()
    _L0_c = _w((lambda *s: np.random.randn(*s).astype(np.float32) * 0.05)(4, 128))
    _L0_wmod = _w((lambda *s: np.random.randn(*s).astype(np.float32) * 0.05)(128, 6 * 128) * 128 ** (-0.5))
    _d = {'L0_attn_x': _L0_attn_in['x'], 'L0_attn_time_decay': _L0_attn_in['time_decay'], 'L0_attn_time_first': _L0_attn_in['time_first'], 'L0_attn_time_mix_k': _L0_attn_in['time_mix_k'], 'L0_attn_time_mix_v': _L0_attn_in['time_mix_v'], 'L0_attn_time_mix_r': _L0_attn_in['time_mix_r'], 'L0_attn_Wk': _L0_attn_in['Wk'], 'L0_attn_Wv': _L0_attn_in['Wv'], 'L0_attn_Wr': _L0_attn_in['Wr'], 'L0_attn_Wo': _L0_attn_in['Wo'], 'L0_ffn_wf': _L0_ffn_in['wf'], 'L0_ffn_uf': _L0_ffn_in['uf'], 'L0_ffn_bf': _L0_ffn_in['bf'], 'L0_ffn_wi': _L0_ffn_in['wi'], 'L0_ffn_ui': _L0_ffn_in['ui'], 'L0_ffn_bi': _L0_ffn_in['bi'], 'L0_ffn_wc': _L0_ffn_in['wc'], 'L0_ffn_uc': _L0_ffn_in['uc'], 'L0_ffn_bc': _L0_ffn_in['bc'], 'L0_ffn_wo': _L0_ffn_in['wo'], 'L0_ffn_uo': _L0_ffn_in['uo'], 'L0_ffn_bo': _L0_ffn_in['bo'], 'L0_ffn_in_c': _L0_ffn_in['in_c'], 'L0_c': _L0_c, 'L0_wmod': _L0_wmod}
    _x0 = _d['L0_attn_x']
    _d['L0_attn_x'] = jax.random.normal(jax.random.fold_in(jax.random.key(seed), 1), (4, 1024, 128), dtype=_x0.dtype)
    del _x0
    return _d

def reference(L0_attn_x, L0_attn_time_decay, L0_attn_time_first, L0_attn_time_mix_k, L0_attn_time_mix_v, L0_attn_time_mix_r, L0_attn_Wk, L0_attn_Wv, L0_attn_Wr, L0_attn_Wo, L0_ffn_wf, L0_ffn_uf, L0_ffn_bf, L0_ffn_wi, L0_ffn_ui, L0_ffn_bi, L0_ffn_wc, L0_ffn_uc, L0_ffn_bc, L0_ffn_wo, L0_ffn_uo, L0_ffn_bo, L0_ffn_in_c, L0_c, L0_wmod):

    def _L0_attn_ref(x, time_decay, time_first, time_mix_k, time_mix_v, time_mix_r, Wk, Wv, Wr, Wo):
        import jax, jax.numpy as jnp
        import numpy as np
        B, T, C = (8, 512, 128)

        def _wkv(w_decay, u_first, k, v):
            w = -jnp.exp(w_decay)
            u = u_first
            kt = jnp.transpose(k, (1, 0, 2))
            vt = jnp.transpose(v, (1, 0, 2))
            a0 = jnp.zeros((k.shape[0], k.shape[2]), dtype=k.dtype)
            b0 = jnp.zeros_like(a0)
            p0 = jnp.full_like(a0, -1e+38)

            def step(carry, kv):
                a, b, p = carry
                k_t, v_t = kv
                q = jnp.maximum(p, u + k_t)
                e1 = jnp.exp(p - q)
                e2 = jnp.exp(u + k_t - q)
                y = (e1 * a + e2 * v_t) / (e1 * b + e2)
                q2 = jnp.maximum(p + w, k_t)
                f1 = jnp.exp(p + w - q2)
                f2 = jnp.exp(k_t - q2)
                return ((f1 * a + f2 * v_t, f1 * b + f2, q2), y)
            _, y = jax.lax.scan(step, (a0, b0, p0), (kt, vt))
            return jnp.transpose(y, (1, 0, 2))
        x_prev = jnp.pad(x, ((0, 0), (1, 0), (0, 0)))[:, :-1]
        xk = x_prev + time_mix_k * (x - x_prev)
        xv = x_prev + time_mix_v * (x - x_prev)
        xr = x_prev + time_mix_r * (x - x_prev)
        k = jnp.einsum('btc,dc->btd', xk, Wk)
        v = jnp.einsum('btc,dc->btd', xv, Wv)
        sr = jax.nn.sigmoid(jnp.einsum('btc,dc->btd', xr, Wr))
        wkv = _wkv(time_decay.reshape(-1), time_first.reshape(-1), k, v)
        return jnp.einsum('btc,dc->btd', sr * wkv, Wo)

    def _L0_ffn_ref(x, wf, uf, bf, wi, ui, bi, wc, uc, bc, wo, uo, bo, in_c):
        import jax, jax.numpy as jnp
        import numpy as np
        from jax import lax
        T, B, I, M, O = (32, 64, 128, 128, 128)

        def _xavier(key, shape):
            fan_out, fan_in = shape
            limit = float(np.sqrt(6.0 / (fan_in + fan_out)))
            return jax.random.uniform(key, shape, jnp.float32, -limit, limit)
        batch = x.shape[1]
        c0 = jnp.broadcast_to(in_c, (batch, in_c.shape[0]))

        def step(c, xt):
            ft = jax.nn.sigmoid(xt @ wf.T + c @ uf.T + bf)
            it = jax.nn.sigmoid(xt @ wi.T + c @ ui.T + bi)
            gt = jnp.tanh(xt @ wc.T + c @ uc.T + bc)
            c = ft * c + it * gt
            return (c, None)
        c_final, _ = lax.scan(step, c0, x)
        h = jnp.tanh(jnp.einsum('tbi,oi->tbo', x, wo) + c_final @ uo.T + bo)
        return h
    x = L0_attn_x
    mod = (_silu(L0_c) @ L0_wmod).reshape(L0_c.shape[0], 6, 1, -1)
    sa, ca, ga, sb, cb, gb = (mod[:, 0], mod[:, 1], mod[:, 2], mod[:, 3], mod[:, 4], mod[:, 5])
    ga = (2 * (ga >= 0) - 1) * jnp.maximum(jnp.abs(ga), 0.25)
    gb = (2 * (gb >= 0) - 1) * jnp.maximum(jnp.abs(gb), 0.25)
    h = _layernorm(x, axis=-1) * (1 + ca) + sa
    x = x + ga * _L0_attn_ref(h, L0_attn_time_decay, L0_attn_time_first, L0_attn_time_mix_k, L0_attn_time_mix_v, L0_attn_time_mix_r, L0_attn_Wk, L0_attn_Wv, L0_attn_Wr, L0_attn_Wo)
    h = _layernorm(x, axis=-1) * (1 + cb) + sb
    x = x + gb * _L0_ffn_ref(h, L0_ffn_wf, L0_ffn_uf, L0_ffn_bf, L0_ffn_wi, L0_ffn_ui, L0_ffn_bi, L0_ffn_wc, L0_ffn_uc, L0_ffn_bc, L0_ffn_wo, L0_ffn_uo, L0_ffn_bo, L0_ffn_in_c)
    return x

_drawn_inputs = setup_inputs


def setup_inputs(seed=0):
    import zlib

    import numpy as np

    out = dict(_drawn_inputs(seed))
    spreads = {'L0_ffn_bf': (0.0, 2.0),
     'L0_ffn_bi': (0.0, 2.0),
     'L0_ffn_bc': (0.0, 0.794),
     'L0_ffn_bo': (0.0, 0.497),
     'L0_ffn_in_c': (0.0, 0.8)}
    factors = {'L0_attn_time_decay': 23.424,
     'L0_attn_time_first': 6.362,
     'L0_attn_time_mix_k': 2.702,
     'L0_attn_time_mix_r': 3.42,
     'L0_ffn_wf': 3.274,
     'L0_ffn_uf': 6.933,
     'L0_ffn_ui': 4.797}
    for name, (base, spread) in spreads.items():
        noise = np.random.default_rng([zlib.crc32(name.encode()), seed]).standard_normal(out[name].shape)
        drawn = base * np.exp(spread * noise) if base else spread * noise
        out[name] = jnp.asarray(drawn.astype(out[name].dtype))
    for name, factor in factors.items():
        out[name] = (out[name] * factor).astype(out[name].dtype)
    return out
```

```python
from contextlib import ExitStack

import concourse.bass as bass
from concourse import mybir

F32 = mybir.dt.float32
ALU = mybir.AluOpType
ACT = mybir.ActivationFunctionType

C = 128
P = 128
NT = 512
J = NT // P
EPS = 1e-5
CAP = float(2 ** 62)
GATE_MIN = 0.25

DECAY, FIRST, MIXK, MIXV, MIXR, BF, BI, BC, BO, INC, COND = range(11)
SA, CA, GA, SB, CB, GB = range(6)


def adaln_rwkv_block_kernel(nc, x, decay, first, mixk, mixv, mixr, wk, wv, wr, wo_att,
                            wf, uf, bf, wi, ui, bi, wc, uc, bc, wo, uo, bo, in_c, cond, wmod, out):
    B, T, _ = x.shape
    CPB = T // NT
    N = B * CPB

    x_d = x.rearrange("b (c p j) d -> p (b c) (j d)", c=CPB, j=J)
    out_d = out.rearrange("b (c p j) d -> p (b c) (j d)", c=CPB, j=J)

    with ExitStack() as ctx:
        def sb(name, shape):
            return ctx.enter_context(nc.sbuf_tensor(name, shape, F32))

        def sem(name):
            return ctx.enter_context(nc.semaphore(name))

        ident = sb("ident", [P, P])
        rows = sb("rows", [P, C])
        cols = sb("cols", [P, 16])
        wmod_sb = sb("wmod_sb", [P, 6 * C])
        w_nat = sb("w_nat", [P, 12, C])
        KW, VW, RW, OW, WF, WI, WC, WOF, UF, UI, UC, UOF = range(12)
        w_now = sb("w_now", [P, 3, C])
        w_prev = sb("w_prev", [P, 3, C])
        wo_g = sb("wo_g", [P, B, C])
        wo_gT = sb("wo_gT", [P, B * C])
        w_ffn = sb("w_ffn", [P, 4, C])
        u_ffn = sb("u_ffn", [P, 4, C])
        one_minus = sb("one_minus", [P, 3])
        w_col = sb("w_col", [P, 1])
        w_full = sb("w_full", [P, NT])
        eps_col = sb("eps_col", [P, 1])
        silu_e = sb("silu_e", [P, B])
        silu = sb("silu", [P, B])
        mods = sb("mods", [P, 6 * B])
        neg_g = sb("neg_g", [P, 6 * B])
        sign_g = sb("sign_g", [P, 6 * B])
        gates = sb("gates", [P, 6 * B])
        bias_t = sb("bias_t", [P, 3])
        bias_0 = sb("bias_0", [P, 3])
        c2_0 = sb("c2_0", [P, 1])

        xs = sb("xs", [P, N, J * C])
        h2 = sb("h2", [P, N, NT])
        hh = sb("hh", [P, 2, T + 1])
        pp = sb("pp", [P, 2, T + 1])
        aa = sb("aa", [P, 2, T + 1])
        bb = sb("bb", [P, 2, T + 1])
        st1 = sb("st1", [P, 2, J, 6])
        mv1 = sb("mv1", [P, 2, J, 2])
        lv1 = sb("lv1", [P, 2, J])
        nm1 = sb("nm1", [P, 2, J])
        rs1 = sb("rs1", [P, 2, J])
        xn1 = sb("xn1", [P, 2, J * C])
        vs = sb("vs", [P, 2, NT])
        er = sb("er", [P, 2, NT])
        d1 = sb("d1", [P, 2, NT])
        d2 = sb("d2", [P, 2, NT])
        d3 = sb("d3", [P, 2, NT])
        f2v = sb("f2v", [P, 2, NT])
        den = sb("den", [P, 2, NT])
        num = sb("num", [P, 2, NT])
        st2 = sb("st2", [P, 2, J, 6])
        mv2 = sb("mv2", [P, 2, J, 2])
        lv2 = sb("lv2", [P, 2, J])
        rs2 = sb("rs2", [P, 2, J])
        nr2 = sb("nr2", [P, 2, J])
        xn2 = sb("xn2", [P, 2, J * C])
        tf = sb("tf", [P, CPB, NT])
        ti = sb("ti", [P, CPB, NT])
        tg = sb("tg", [P, CPB, NT])
        c2 = sb("c2", [P, CPB, NT])
        uoc = sb("uoc", [P, CPB, NT])
        pre = sb("pre", [P, 2, NT])

        banks = [ctx.enter_context(nc.psum_tensor(f"bank{i}", [P, NT], F32)) for i in range(8)]
        T1_PS, K_PS, V_PS, R_PS, WO_PS, T2_PS = banks[0], banks[1:3], banks[3], banks[4], banks[5], banks[6]
        SETUP_PS = banks[7]
        G_PS = [banks[0:3], banks[3:6]]
        FIN_PS, OT_PS = banks[6], banks[7]

        names = ("ident_set zero_set rows_in small_in cond_in cols_ps cols_sb silu_exp silu_up silu_ready mod_ps mods_sb "
                 "decay_exp w_ready eps_set neg_ready gates_ready wog_ready wT_ps wT_used mix_ready kvr_w wogT_ready "
                 "ffn_w u_bias_ps bias_ready edges_set "
                 "stats1a stats1 lnvar1 rstd1 xn1_ready t1_done h_ready k_done v_done r_done "
                 "p_start p_ready d1_ready d2_ready d3_ready f1_ready f2_ready e_ready v_ready er_ready erc_ready "
                 "b_ready f2v_ready a_ready den_ready wv_ready num_ready lr_ready ld_ready logs_ready rg_ready "
                 "y_ready wo_done x2_ready stats2a stats2 lnvar2 rstd2 nr2_ready xn2_ready t2_done h2_ready "
                 "gate_ps tf_ready ti_ready tg_ready ig_ready fc_ready c_ready uoc_ps uoc_ready fin_ps pre_ready "
                 "hf_ready hg_ready ot_done out_ready stored wmod_in").split()
        S = {n: sem(n) for n in names}
        x_in = [sem(f"x_in{i}") for i in range(N)]
        w_in = [sem(f"w_in{i}") for i in range(12)]

        def col(n):
            return cols[:, n:n + 1]

        def mod(s, b):
            return mods[:, s * B + b:s * B + b + 1]

        def gate(s, b):
            return gates[:, s * B + b:s * B + b + 1]

        def at(c):
            return (c // CPB) % 2, (c % CPB) * NT

        block = ctx.enter_context(nc.Block())

        def pipeline(stages, first, last):
            for i in range(first, last):
                for stage, lead in stages:
                    if 0 <= i + lead < N:
                        stage(i + lead)

        FIRST_TICK, LAST_TICK = -3, N + 4
        STEPS = [(t, q) for t in range(B) for q in range(CPB)]
        FINALS = [(q, t) for q in range(CPB) for t in range(B)]

        @block.sync
        def _(sp):
            sp.wait_ge(S["zero_set"], 1)
            for n, v in ((DECAY, decay), (FIRST, first), (MIXK, mixk), (MIXV, mixv), (MIXR, mixr)):
                sp.dma_start(rows[n:n + 1, :], v.rearrange("a b d -> (a b) d")).then_inc(S["rows_in"], 16)
            for n, v in ((BF, bf), (BI, bi), (BC, bc), (BO, bo), (INC, in_c)):
                sp.dma_start(rows[n:n + 1, :], v.rearrange("(a d) -> a d", a=1)).then_inc(S["rows_in"], 16)
            sp.dma_start(rows[COND:COND + B, :], cond).then_inc(S["rows_in"], 16)
            for c in range(N):
                sp.dma_start(xs[:, c, :], x_d[:, c, :]).then_inc(x_in[c], 16)
            for n, (q, t) in enumerate(FINALS):
                c = t * CPB + q
                sp.wait_ge(S["out_ready"], n + 1)
                sp.dma_start(out_d[:, c, :], xs[:, c, :]).then_inc(S["stored"], 16)
            sp.wait_ge(S["stored"], 16 * N)

        @block.gpsimd
        def _(pool):
            g = nc.gpsimd
            g.memset(ident[:], 0.0).then_inc(S["ident_set"], 1)
            g.memset(rows[:], 0.0).then_inc(S["zero_set"], 1)
            pool.wait_ge(S["ident_set"], 1)
            g.affine_select(out=ident[:], in_=ident[:], compare_op=ALU.not_equal, fill=1.0, base=0,
                            pattern=[[-1, P]], channel_multiplier=1).then_inc(S["ident_set"], 1)
            for tile, v in ((hh, 0.0), (aa, 0.0), (bb, 0.0)):
                for k in range(2):
                    last = g.memset(tile[:, k, 0:1], v)
                    last.then_inc(S["edges_set"], 1)

            def norm1(c):
                k = c % 2
                pool.wait_ge(S["rstd1"], c + 1)
                if c >= 2:
                    pool.wait_ge(S["t1_done"], c - 1)
                for j in range(J):
                    last = g.tensor_scalar(xn1[:, k, j * C:(j + 1) * C], xs[:, c, j * C:(j + 1) * C],
                                           nm1[:, k, j:j + 1], rs1[:, k, j:j + 1], ALU.add, ALU.mult)
                last.then_inc(S["xn1_ready"], 1)

            def decay_step(c):
                k, (m, o) = c % 2, at(c)
                pool.wait_ge(S["p_ready"], c + 1)
                if c >= 2:
                    pool.wait_ge(S["a_ready"], c - 1)
                g.tensor_tensor(d1[:, k, :], pp[:, m, o:o + NT], pp[:, m, o + 1:o + 1 + NT],
                                ALU.subtract).then_inc(S["d1_ready"], 1)

            def weigh_v(c):
                k = c % 2
                pool.wait_ge(S["f2_ready"], c + 1)
                pool.wait_ge(S["v_ready"], c + 1)
                if c >= 2:
                    pool.wait_ge(S["a_ready"], c - 1)
                g.tensor_tensor(f2v[:, k, :], d2[:, k, :], vs[:, k, :], ALU.mult).then_inc(S["f2v_ready"], 1)

            def cap_r(c):
                k = c % 2
                pool.wait_ge(S["er_ready"], c + 1)
                g.tensor_scalar(er[:, k, :], er[:, k, :], CAP, 0.0, ALU.min, ALU.max).then_inc(S["erc_ready"], 1)

            def add_a(c):
                k, (m, o) = c % 2, at(c)
                pool.wait_ge(S["wv_ready"], c + 1)
                pool.wait_ge(S["a_ready"], c + 1)
                g.tensor_tensor(num[:, k, :], num[:, k, :], aa[:, m, o:o + NT], ALU.add).then_inc(S["num_ready"], 1)

            def make_y(c):
                k = c % 2
                pool.wait_ge(S["num_ready"], c + 1)
                pool.wait_ge(S["rg_ready"], c + 1)
                g.tensor_tensor(num[:, k, :], num[:, k, :], den[:, k, :], ALU.mult).then_inc(S["y_ready"], 1)

            pipeline([(decay_step, 0), (make_y, -1), (weigh_v, 0), (norm1, 2), (cap_r, 0), (add_a, 0)],
                     FIRST_TICK, LAST_TICK)

        @block.scalar
        def _(act):
            a = nc.scalar
            for n, v in ((KW, wk), (VW, wv), (RW, wr), (OW, wo_att)):
                act.dma_start(w_nat[:, n, :], v).then_inc(w_in[n], 16)
            act.dma_start(wmod_sb[:], wmod).then_inc(S["wmod_in"], 16)
            for n, v in ((WF, wf), (WI, wi), (WC, wc), (WOF, wo), (UF, uf), (UI, ui), (UC, uc), (UOF, uo)):
                act.dma_start(w_nat[:, n, :], v).then_inc(w_in[n], 16)
            act.wait_ge(S["cols_sb"], 1)
            a.activation(silu_e[:], cols[:, COND:COND + B], ACT.Exp, scale=-1.0).then_inc(S["silu_exp"], 1)
            a.activation(w_col[:], col(DECAY), ACT.Exp).then_inc(S["decay_exp"], 1)

            def rstd1(c):
                k = c % 2
                act.wait_ge(S["stats1"], c + 1)
                if c == 0:
                    act.wait_ge(S["eps_set"], 1)
                if c >= 2:
                    act.wait_ge(S["xn1_ready"], c - 1)
                a.activation(lv1[:, k, :], mv1[:, k, :, 1], ACT.Ln, bias=eps_col[:, 0:1]).then_inc(S["lnvar1"], 1)
                a.mul(nm1[:, k, :], mv1[:, k, :, 0], -1.0)
                act.wait_ge(S["lnvar1"], c + 1)
                a.activation(rs1[:, k, :], lv1[:, k, :], ACT.Exp, scale=-0.5).then_inc(S["rstd1"], 1)

            def evac_h(c):
                m, o = at(c)
                act.wait_ge(S["t1_done"], c + 1)
                if c == 0:
                    act.wait_ge(S["mods_sb"], 2)
                    act.wait_ge(S["edges_set"], 6)
                if c >= 2 * CPB:
                    act.wait_ge(S["r_done"], c - 2 * CPB + 1)
                a.activation(hh[:, m, o + 1:o + 1 + NT].rearrange("q (p j) -> q p j", j=J),
                             T1_PS[:, :].rearrange("q (j p) -> q p j", j=J), ACT.Identity,
                             scale=mod(CA, c // CPB), bias=mod(SA, c // CPB)).then_inc(S["h_ready"], 1)

            def evac_v(c):
                k = c % 2
                act.wait_ge(S["v_done"], c + 1)
                if c >= 2:
                    act.wait_ge(S["wv_ready"], c - 1)
                    act.wait_ge(S["f2v_ready"], c - 1)
                a.copy(vs[:, k, :], V_PS[:, :]).then_inc(S["v_ready"], 1)

            def exp_r(c):
                k = c % 2
                act.wait_ge(S["r_done"], c + 1)
                if c >= 2:
                    act.wait_ge(S["logs_ready"], c - 1)
                a.activation(er[:, k, :], R_PS[:, :], ACT.Exp, scale=-1.0).then_inc(S["er_ready"], 1)

            def exps(c):
                k = c % 2
                act.wait_ge(S["d2_ready"], c + 1)
                a.activation(d2[:, k, :], d2[:, k, :], ACT.Exp).then_inc(S["f2_ready"], 1)
                act.wait_ge(S["d3_ready"], c + 1)
                a.activation(d3[:, k, :], d3[:, k, :], ACT.Exp, bias=col(FIRST)).then_inc(S["e_ready"], 1)
                act.wait_ge(S["d1_ready"], c + 1)
                a.activation(d1[:, k, :], d1[:, k, :], ACT.Exp, bias=w_col[:, 0:1]).then_inc(S["f1_ready"], 1)

            def ln_r(c):
                k = c % 2
                act.wait_ge(S["erc_ready"], c + 1)
                a.activation(er[:, k, :], er[:, k, :], ACT.Ln, bias=1.0).then_inc(S["lr_ready"], 1)

            def ln_den(c):
                k = c % 2
                act.wait_ge(S["den_ready"], c + 1)
                a.activation(den[:, k, :], den[:, k, :], ACT.Ln).then_inc(S["ld_ready"], 1)

            def exp_rg(c):
                k = c % 2
                act.wait_ge(S["logs_ready"], c + 1)
                a.activation(den[:, k, :], den[:, k, :], ACT.Exp, scale=-1.0).then_inc(S["rg_ready"], 1)

            def rstd2(c):
                k = c % 2
                act.wait_ge(S["stats2"], c + 1)
                if c >= 2:
                    act.wait_ge(S["nr2_ready"], c - 1)
                a.activation(lv2[:, k, :], mv2[:, k, :, 1], ACT.Ln, bias=eps_col[:, 0:1]).then_inc(S["lnvar2"], 1)
                act.wait_ge(S["lnvar2"], c + 1)
                a.activation(rs2[:, k, :], lv2[:, k, :], ACT.Exp, scale=-0.5).then_inc(S["rstd2"], 1)

            def norm2(c):
                k = c % 2
                act.wait_ge(S["nr2_ready"], c + 1)
                if c >= 2:
                    act.wait_ge(S["t2_done"], c - 1)
                for j in range(J):
                    last = a.activation(xn2[:, k, j * C:(j + 1) * C], xs[:, c, j * C:(j + 1) * C], ACT.Identity,
                                        scale=rs2[:, k, j:j + 1], bias=nr2[:, k, j:j + 1])
                last.then_inc(S["xn2_ready"], 1)

            def evac_h2(c):
                act.wait_ge(S["t2_done"], c + 1)
                a.activation(h2[:, c, :], T2_PS[:, :], ACT.Identity, scale=mod(CB, c // CPB),
                             bias=mod(SB, c // CPB)).then_inc(S["h2_ready"], 1)

            act.wait_ge(S["w_ready"], 1)
            pipeline([(exps, 0), (exp_rg, -1), (rstd1, 2), (evac_h, 1), (norm2, -2), (evac_v, 1), (exp_r, 1),
                      (evac_h2, -2), (ln_r, 0), (ln_den, 0), (rstd2, -1)], FIRST_TICK, LAST_TICK)

            for n, (t, q) in enumerate(STEPS):
                bias = bias_t if t else bias_0
                act.wait_ge(S["gate_ps"], 3 * n + 1)
                if n == 0:
                    act.wait_ge(S["bias_ready"], 2)
                if t:
                    act.wait_ge(S["fc_ready"], n - CPB + 1)
                a.activation(tf[:, q, :], G_PS[q][0][:, :], ACT.Tanh, scale=0.5,
                             bias=bias[:, 0:1]).then_inc(S["tf_ready"], 1)
                act.wait_ge(S["gate_ps"], 3 * n + 2)
                if t:
                    act.wait_ge(S["c_ready"], n - CPB + 1)
                a.activation(ti[:, q, :], G_PS[q][1][:, :], ACT.Tanh, scale=0.5,
                             bias=bias[:, 1:2]).then_inc(S["ti_ready"], 1)
                act.wait_ge(S["gate_ps"], 3 * n + 3)
                a.activation(tg[:, q, :], G_PS[q][2][:, :], ACT.Tanh,
                             bias=bias[:, 2:3]).then_inc(S["tg_ready"], 1)
            for n, (q, t) in enumerate(FINALS):
                k = n % 2
                if t == 0:
                    act.wait_ge(S["uoc_ps"], q + 1)
                    a.activation(uoc[:, q, :], G_PS[q][0][:, :], ACT.Identity, bias=col(BO)).then_inc(S["uoc_ready"], 1)
                act.wait_ge(S["pre_ready"], n + 1)
                a.activation(pre[:, k, :], pre[:, k, :], ACT.Tanh).then_inc(S["hf_ready"], 1)

        @block.vector
        def _(dve):
            v = nc.vector
            v.memset(eps_col[:], EPS).then_inc(S["eps_set"], 1)
            v.memset(w_full[:], 0.0).then_inc(S["eps_set"], 1)
            dve.wait_ge(S["cols_ps"], 1)
            v.tensor_copy(cols[:], SETUP_PS[:, 0:16]).then_inc(S["cols_sb"], 1)
            dve.wait_ge(S["silu_exp"], 1)
            v.tensor_scalar(silu_e[:], silu_e[:], 1.0, None, ALU.add).then_inc(S["silu_up"], 1)
            dve.wait_ge(S["silu_up"], 1)
            v.reciprocal(silu_e[:], silu_e[:]).then_inc(S["silu_up"], 1)
            dve.wait_ge(S["silu_up"], 2)
            v.tensor_tensor(silu[:], silu_e[:], cols[:, COND:COND + B], ALU.mult).then_inc(S["silu_ready"], 1)
            v.tensor_scalar(one_minus[:], cols[:, MIXK:MIXR + 1], -1.0, 1.0, ALU.mult, ALU.add).then_inc(S["mix_ready"], 1)
            dve.wait_ge(S["decay_exp"], 1)
            v.tensor_scalar(w_col[:], w_col[:], -1.0, None, ALU.mult).then_inc(S["w_ready"], 1)
            dve.wait_ge(S["w_ready"], 1)
            dve.wait_ge(S["eps_set"], 2)
            v.tensor_scalar(w_full[:], w_full[:], w_col[:, 0:1], None, ALU.add).then_inc(S["w_ready"], 1)
            dve.wait_ge(S["mod_ps"], 1)
            v.tensor_copy(mods[:], SETUP_PS[:, 16:16 + 6 * B]).then_inc(S["mods_sb"], 1)
            dve.wait_ge(S["mods_sb"], 1)
            v.tensor_scalar(neg_g[:], mods[:], -1.0, None, ALU.mult).then_inc(S["neg_ready"], 1)
            v.tensor_scalar(sign_g[:], mods[:], 0.0, 2.0, ALU.is_ge, ALU.mult).then_inc(S["neg_ready"], 1)
            dve.wait_ge(S["neg_ready"], 2)
            v.scalar_tensor_tensor(out=neg_g[:], in0=neg_g[:], scalar=GATE_MIN, in1=mods[:], op0=ALU.max,
                                   op1=ALU.max).then_inc(S["neg_ready"], 1)
            dve.wait_ge(S["neg_ready"], 3)
            v.scalar_tensor_tensor(out=gates[:], in0=sign_g[:], scalar=-1.0, in1=neg_g[:], op0=ALU.add,
                                   op1=ALU.mult).then_inc(S["gates_ready"], 1)
            m2 = mods[:, :].rearrange("p (h s b) -> p h s b", h=2, s=3)[:, :, CA, :]
            v.tensor_scalar(m2, m2, 1.0, None, ALU.add).then_inc(S["mods_sb"], 1)

            def kvr_weights():
                dve.wait_ge(S["mix_ready"], 1)
                dve.wait_ge(S["wT_ps"], 1)
                for n in range(3):
                    v.tensor_scalar(w_now[:, n, :], K_PS[0][:, n * C:(n + 1) * C], col(MIXK + n), None, ALU.mult)
                    last = v.tensor_scalar(w_prev[:, n, :], K_PS[0][:, n * C:(n + 1) * C], one_minus[:, n:n + 1],
                                           None, ALU.mult)
                last.then_inc(S["kvr_w"], 1)

            def gate_wo():
                dve.wait_ge(S["gates_ready"], 1)
                dve.wait_ge(w_in[OW], 16)
                for b in range(B):
                    last = v.tensor_scalar(wo_g[:, b, :], w_nat[:, OW, :], gate(GA, b), None, ALU.mult)
                last.then_inc(S["wog_ready"], 1)

            def later_weights():
                dve.wait_ge(S["wT_ps"], 2)
                v.tensor_copy(wo_gT[:], WO_PS[:, :]).then_inc(S["wogT_ready"], 1)
                dve.wait_ge(S["wT_ps"], 3)
                v.tensor_copy(w_ffn[:, :, :], T2_PS[:, :].rearrange("p (n c) -> p n c", n=4)).then_inc(S["ffn_w"], 1)
                dve.wait_ge(S["wT_ps"], 4)
                v.tensor_scalar(u_ffn[:, :, :], SETUP_PS[:, :].rearrange("p (n c) -> p n c", n=4), 0.5, None,
                                ALU.mult).then_inc(S["ffn_w"], 1)
                v.tensor_scalar(c2_0[:], col(INC), 2.0, None, ALU.mult).then_inc(S["ffn_w"], 1)
                v.tensor_scalar(bias_t[:, 0:2], cols[:, BF:BI + 1], 0.5, None, ALU.mult).then_inc(S["bias_ready"], 1)
                v.tensor_copy(bias_t[:, 2:3], col(BC)).then_inc(S["bias_ready"], 1)

            def first_bias():
                dve.wait_ge(S["u_bias_ps"], 1)
                dve.wait_ge(S["bias_ready"], 2)
                v.scalar_tensor_tensor(out=bias_0[:, 0:2], in0=SETUP_PS[:, 0:2], scalar=0.5, in1=bias_t[:, 0:2],
                                       op0=ALU.mult, op1=ALU.add)
                v.tensor_tensor(bias_0[:, 2:3], SETUP_PS[:, 2:3], bias_t[:, 2:3], ALU.add).then_inc(S["bias_ready"], 1)

            def token_stats(c, st, mv, part, ready):
                k = c % 2
                for j in range(J):
                    last = v.bn_stats(st[:, k, j, :], xs[:, c, j * C:(j + 1) * C])
                last.then_inc(part, 1)
                dve.wait_ge(part, c + 1)
                for j in range(J):
                    last = v.bn_aggr(mv[:, k, j, :], st[:, k, j, :])
                last.then_inc(ready, 1)

            def stats1(c):
                dve.wait_ge(x_in[c], 16)
                if c >= 2:
                    dve.wait_ge(S["rstd1"], c - 1)
                token_stats(c, st1, mv1, S["stats1a"], S["stats1"])

            def run_max(c):
                k, (m, o) = c % 2, at(c)
                dve.wait_ge(S["k_done"], c + 1)
                if c == 0:
                    dve.wait_ge(S["w_ready"], 2)
                    dve.wait_ge(S["edges_set"], 6)
                else:
                    dve.wait_ge(S["p_ready"], c)
                if c % CPB == 0:
                    v.tensor_copy(pp[:, m, 0:1], K_PS[k][:, 0:1]).then_inc(S["p_start"], 1)
                    dve.wait_ge(S["p_start"], c // CPB + 1)
                v.tensor_tensor_scan(pp[:, m, o + 1:o + 1 + NT], w_full[:], K_PS[k][:, :], pp[:, m, o:o + 1],
                                     ALU.add, ALU.max).then_inc(S["p_ready"], 1)
                dve.wait_ge(S["p_ready"], c + 1)
                if c >= 2:
                    dve.wait_ge(S["f2v_ready"], c - 1)
                v.tensor_tensor(d2[:, k, :], K_PS[k][:, :], pp[:, m, o + 1:o + 1 + NT],
                                ALU.subtract).then_inc(S["d2_ready"], 1)
                v.tensor_tensor(d3[:, k, :], K_PS[k][:, :], pp[:, m, o:o + NT],
                                ALU.subtract).then_inc(S["d3_ready"], 1)

            def states(c):
                k, (m, o) = c % 2, at(c)
                dve.wait_ge(S["f1_ready"], c + 1)
                dve.wait_ge(S["f2_ready"], c + 1)
                v.tensor_tensor_scan(bb[:, m, o + 1:o + 1 + NT], d1[:, k, :], d2[:, k, :], bb[:, m, o:o + 1],
                                     ALU.mult, ALU.add).then_inc(S["b_ready"], 1)
                dve.wait_ge(S["e_ready"], c + 1)
                dve.wait_ge(S["v_ready"], c + 1)
                if c >= 2:
                    dve.wait_ge(S["wo_done"], c - 1)
                v.scalar_tensor_tensor(out=num[:, k, :], in0=d3[:, k, :], scalar=CAP, in1=vs[:, k, :],
                                       op0=ALU.min, op1=ALU.mult).then_inc(S["wv_ready"], 1)
                dve.wait_ge(S["b_ready"], c + 1)
                if c >= 2:
                    dve.wait_ge(S["y_ready"], c - 1)
                v.scalar_tensor_tensor(out=den[:, k, :], in0=d3[:, k, :], scalar=CAP, in1=bb[:, m, o:o + NT],
                                       op0=ALU.min, op1=ALU.add).then_inc(S["den_ready"], 1)
                dve.wait_ge(S["f2v_ready"], c + 1)
                v.tensor_tensor_scan(aa[:, m, o + 1:o + 1 + NT], d1[:, k, :], f2v[:, k, :], aa[:, m, o:o + 1],
                                     ALU.mult, ALU.add).then_inc(S["a_ready"], 1)

            def add_logs(c):
                k = c % 2
                dve.wait_ge(S["lr_ready"], c + 1)
                dve.wait_ge(S["ld_ready"], c + 1)
                v.tensor_tensor(den[:, k, :], den[:, k, :], er[:, k, :], ALU.add).then_inc(S["logs_ready"], 1)

            def residual(c):
                dve.wait_ge(S["wo_done"], c + 1)
                v.tensor_tensor(xs[:, c, :], WO_PS[:, :], xs[:, c, :], ALU.add).then_inc(S["x2_ready"], 1)
                dve.wait_ge(S["x2_ready"], c + 1)
                if c >= 2:
                    dve.wait_ge(S["nr2_ready"], c - 1)
                token_stats(c, st2, mv2, S["stats2a"], S["stats2"])

            def minus_mean2(c):
                k = c % 2
                dve.wait_ge(S["rstd2"], c + 1)
                if c >= 2:
                    dve.wait_ge(S["xn2_ready"], c - 1)
                v.scalar_tensor_tensor(out=nr2[:, k, :], in0=mv2[:, k, :, 0], scalar=-1.0, in1=rs2[:, k, :],
                                       op0=ALU.mult, op1=ALU.mult).then_inc(S["nr2_ready"], 1)

            def stage0(c):
                stats1(c)
                if c == 0:
                    kvr_weights()
                    gate_wo()
                if c == 1:
                    later_weights()
                if c == 2:
                    first_bias()

            pipeline([(run_max, 0), (add_logs, -1), (minus_mean2, -2), (stage0, 2), (states, 0),
                      (residual, -1)], FIRST_TICK, LAST_TICK)

            for n, (t, q) in enumerate(STEPS):
                dve.wait_ge(S["tf_ready"], n + 1)
                if t:
                    dve.wait_ge(S["c_ready"], n - CPB + 1)
                    v.scalar_tensor_tensor(out=tf[:, q, :], in0=tf[:, q, :], scalar=1.0, in1=c2[:, q, :],
                                           op0=ALU.add, op1=ALU.mult).then_inc(S["fc_ready"], 1)
                else:
                    dve.wait_ge(S["ffn_w"], 3)
                    v.tensor_scalar(tf[:, q, :], tf[:, q, :], 1.0, c2_0[:, 0:1], ALU.add,
                                    ALU.mult).then_inc(S["fc_ready"], 1)
                dve.wait_ge(S["ti_ready"], n + 1)
                dve.wait_ge(S["tg_ready"], n + 1)
                v.scalar_tensor_tensor(out=ti[:, q, :], in0=ti[:, q, :], scalar=1.0, in1=tg[:, q, :],
                                       op0=ALU.add, op1=ALU.mult).then_inc(S["ig_ready"], 1)
                dve.wait_ge(S["fc_ready"], n + 1)
                dve.wait_ge(S["ig_ready"], n + 1)
                v.scalar_tensor_tensor(out=c2[:, q, :], in0=tf[:, q, :], scalar=0.5, in1=ti[:, q, :],
                                       op0=ALU.mult, op1=ALU.add).then_inc(S["c_ready"], 1)
            def pre_tanh(n):
                q, t = FINALS[n]
                k = n % 2
                dve.wait_ge(S["fin_ps"], n + 1)
                if t == 0:
                    dve.wait_ge(S["uoc_ready"], q + 1)
                if n >= 2:
                    dve.wait_ge(S["ot_done"], n - 1)
                v.tensor_tensor(pre[:, k, :], FIN_PS[:, :], uoc[:, q, :], ALU.add).then_inc(S["pre_ready"], 1)

            def gate_ffn(n):
                q, t = FINALS[n]
                k = n % 2
                dve.wait_ge(S["hf_ready"], n + 1)
                v.tensor_scalar(pre[:, k, :], pre[:, k, :], gate(GB, t), None, ALU.mult).then_inc(S["hg_ready"], 1)

            def output(n):
                q, t = FINALS[n]
                c = t * CPB + q
                dve.wait_ge(S["ot_done"], n + 1)
                v.tensor_tensor(xs[:, c, :], OT_PS[:, :], xs[:, c, :], ALU.add).then_inc(S["out_ready"], 1)

            for n in range(N + 1):
                if n < N:
                    pre_tanh(n)
                if n:
                    output(n - 1)
                if n < N:
                    gate_ffn(n)

        @block.tensor
        def _(pe):
            t_ = nc.tensor
            pe.wait_ge(S["ident_set"], 2)
            pe.wait_ge(S["rows_in"], 16 * 11)
            t_.transpose(SETUP_PS[:, 0:P], rows[:, :], ident[:, :]).then_inc(S["cols_ps"], 1)
            for n in (KW, VW, RW):
                pe.wait_ge(w_in[n], 16)
                last = t_.transpose(K_PS[0][:, n * C:(n + 1) * C], w_nat[:, n, :], ident[:, :])
            last.then_inc(S["wT_ps"], 1)
            pe.wait_ge(S["wmod_in"], 16)
            pe.wait_ge(S["silu_ready"], 1)
            pe.wait_ge(S["cols_sb"], 1)
            for s in range(6):
                last = t_.matmul(SETUP_PS[:, 16 + s * B:16 + (s + 1) * B], wmod_sb[:, s * C:(s + 1) * C], silu[:],
                                 start=True, stop=True)
            last.then_inc(S["mod_ps"], 1)

            def later_weights():
                pe.wait_ge(S["wog_ready"], 1)
                for b in range(B):
                    last = t_.transpose(WO_PS[:, b * C:(b + 1) * C], wo_g[:, b, :], ident[:, :])
                last.then_inc(S["wT_ps"], 1)
                for n in range(4):
                    pe.wait_ge(w_in[WF + n], 16)
                    last = t_.transpose(T2_PS[:, n * C:(n + 1) * C], w_nat[:, WF + n, :], ident[:, :])
                last.then_inc(S["wT_ps"], 1)
                pe.wait_ge(S["mods_sb"], 1)
                for n in range(4):
                    pe.wait_ge(w_in[UF + n], 16)
                    last = t_.transpose(SETUP_PS[:, n * C:(n + 1) * C], w_nat[:, UF + n, :], ident[:, :])
                last.then_inc(S["wT_ps"], 1)

            def first_bias():
                pe.wait_ge(S["ffn_w"], 3)
                for n in range(3):
                    last = t_.matmul(SETUP_PS[:, n:n + 1], u_ffn[:, n, :], c2_0[:], start=True, stop=True)
                last.then_inc(S["u_bias_ps"], 1)

            def turn1(c):
                k = c % 2
                pe.wait_ge(S["xn1_ready"], c + 1)
                if c:
                    pe.wait_ge(S["h_ready"], c)
                for j in range(J):
                    last = t_.transpose(T1_PS[:, j * P:(j + 1) * P], xn1[:, k, j * C:(j + 1) * C], ident[:, :])
                last.then_inc(S["t1_done"], 1)

            def project(c):
                m, o = at(c)
                pe.wait_ge(S["h_ready"], c + 1)
                if c == 0:
                    pe.wait_ge(S["kvr_w"], 1)
                for n, (ps, done, free, least) in enumerate((
                        (K_PS[c % 2], "k_done", "d3_ready", c - 1),
                        (V_PS, "v_done", "v_ready", c),
                        (R_PS, "r_done", "er_ready", c))):
                    if least > 0:
                        pe.wait_ge(S[free], least)
                    t_.matmul(ps[:, :], w_now[:, n, :], hh[:, m, o + 1:o + 1 + NT], start=True, stop=False)
                    t_.matmul(ps[:, :], w_prev[:, n, :], hh[:, m, o:o + NT], start=False,
                              stop=True).then_inc(S[done], 1)

            def project_out(c):
                k = c % 2
                pe.wait_ge(S["y_ready"], c + 1)
                if c == 0:
                    pe.wait_ge(S["wogT_ready"], 1)
                else:
                    pe.wait_ge(S["x2_ready"], c)
                y = num[:, k, :].rearrange("q (p j) -> q j p", j=J)
                b = c // CPB
                for j in range(J):
                    last = t_.matmul(WO_PS[:, j * C:(j + 1) * C], y[:, j, :], wo_gT[:, b * C:(b + 1) * C],
                                     start=True, stop=True)
                last.then_inc(S["wo_done"], 1)

            def turn2(c):
                k = c % 2
                pe.wait_ge(S["xn2_ready"], c + 1)
                if c:
                    pe.wait_ge(S["h2_ready"], c)
                else:
                    pe.wait_ge(S["ffn_w"], 1)
                for j in range(J):
                    last = t_.transpose(T2_PS[:, j * P:(j + 1) * P], xn2[:, k, j * C:(j + 1) * C], ident[:, :])
                last.then_inc(S["t2_done"], 1)

            def stage0(c):
                turn1(c)
                project(c)
                if c == 0:
                    later_weights()
                if c == 1:
                    first_bias()

            pipeline([(stage0, 1), (turn2, -2), (project_out, -1)], FIRST_TICK, LAST_TICK)

            pe.wait_ge(S["h2_ready"], N)
            pe.wait_ge(S["ffn_w"], 3)
            for n, (t, q) in enumerate(STEPS):
                c = t * CPB + q
                for w in range(3):
                    if t:
                        pe.wait_ge(S[("tf_ready", "ti_ready", "tg_ready")[w]], n - CPB + 1)
                    last = t_.matmul(G_PS[q][w][:, :], w_ffn[:, w, :], h2[:, c, :], start=True, stop=(t == 0))
                    if t == 0:
                        last.then_inc(S["gate_ps"], 1)
                if t:
                    pe.wait_ge(S["c_ready"], n - CPB + 1)
                    for w in range(3):
                        t_.matmul(G_PS[q][w][:, :], u_ffn[:, w, :], c2[:, q, :], start=False,
                                  stop=True).then_inc(S["gate_ps"], 1)

            def final(n):
                q, t = FINALS[n]
                c = t * CPB + q
                if t == 0:
                    pe.wait_ge(S["c_ready"], N - CPB + q + 1)
                    t_.matmul(G_PS[q][0][:, :], u_ffn[:, 3, :], c2[:, q, :], start=True,
                              stop=True).then_inc(S["uoc_ps"], 1)
                if n:
                    pe.wait_ge(S["pre_ready"], n)
                t_.matmul(FIN_PS[:, :], w_ffn[:, 3, :], h2[:, c, :], start=True, stop=True).then_inc(S["fin_ps"], 1)

            def turn_back(n):
                k = n % 2
                pe.wait_ge(S["hg_ready"], n + 1)
                if n:
                    pe.wait_ge(S["out_ready"], n)
                for j in range(J):
                    last = t_.transpose(OT_PS[:, j * C:(j + 1) * C], pre[:, k, j * P:(j + 1) * P], ident[:, :])
                last.then_inc(S["ot_done"], 1)

            for n in range(N + 1):
                if n < N:
                    final(n)
                if n:
                    turn_back(n - 1)


_INS = ["L0_attn_x", "L0_attn_time_decay", "L0_attn_time_first", "L0_attn_time_mix_k", "L0_attn_time_mix_v",
        "L0_attn_time_mix_r", "L0_attn_Wk", "L0_attn_Wv", "L0_attn_Wr", "L0_attn_Wo", "L0_ffn_wf", "L0_ffn_uf",
        "L0_ffn_bf", "L0_ffn_wi", "L0_ffn_ui", "L0_ffn_bi", "L0_ffn_wc", "L0_ffn_uc", "L0_ffn_bc", "L0_ffn_wo",
        "L0_ffn_uo", "L0_ffn_bo", "L0_ffn_in_c", "L0_c", "L0_wmod"]


def kernel(**inputs):
    import numpy as _np
    import concourse.bacc as _bacc
    from concourse import mybir as _mybir
    from concourse.bass_utils import run_bass_kernel_spmd as _run

    nc = _bacc.Bacc("TRN2", target_bir_lowering=False, num_devices=1)
    arrays, args = {}, []
    for name in _INS:
        a = _np.ascontiguousarray(inputs[name])
        arrays[f"in_{name}_dram"] = a
        args.append(nc.dram_tensor(f"in_{name}_dram", a.shape, _mybir.dt.from_np(a.dtype), kind="ExternalInput").ap())
    shape = inputs["L0_attn_x"].shape
    args.append(nc.dram_tensor("out_0_dram", shape, F32, kind="ExternalOutput").ap())
    adaln_rwkv_block_kernel(nc, *args)
    r = _run(nc, [arrays], core_ids=[0])
    return r.results[0]["out_0_dram"]
```

```python
from contextlib import ExitStack

import concourse.bass as bass
from concourse import mybir

F32 = mybir.dt.float32
ALU = mybir.AluOpType
ACT = mybir.ActivationFunctionType

C = 128
P = 128
NT = 512
J = NT // P
EPS = 1e-5
CAP = float(2 ** 62)
GATE_MIN = 0.25
WARM_UP = 12
RING = 3

DECAY, FIRST, MIXK, MIXV, MIXR, BF, BI, BC, BO, INC, COND = range(11)
SA, CA, GA, SB, CB, GB = range(6)


WK, WV, WR, WO_ATT, WMOD = range(5)
WF, WI, WC, WO_FFN, UF, UI, UC, UO_FFN = range(8)


def adaln_rwkv_block_kernel(nc, x, small, att_w, ffn_w, out):
    B, T, _ = x.shape
    CPB = T // NT
    N = B * CPB

    x_d = x.rearrange("b (c p j) d -> p (b c) (j d)", c=CPB, j=J)
    out_d = out.rearrange("b (c p j) d -> p (b c) (j d)", c=CPB, j=J)

    with ExitStack() as ctx:
        def sb(name, shape):
            return ctx.enter_context(nc.sbuf_tensor(name, shape, F32))

        def sem(name):
            return ctx.enter_context(nc.semaphore(name))

        ident = sb("ident", [P, P])
        minus_ident = sb("minus_ident", [P, P])
        cols = sb("cols", [P, COND + B])
        w_att = sb("w_att", [P, 10, C])
        w_ffn = sb("w_ffn", [P, 8, C])
        u_half = sb("u_half", [P, 4, C])
        w_now = sb("w_now", [P, 3, C])
        w_prev = sb("w_prev", [P, 3, C])
        wo_g = sb("wo_g", [P, B, C])
        wo_gT = sb("wo_gT", [P, B * C])
        one_minus = sb("one_minus", [P, 3])
        w_col = sb("w_col", [P, 1])
        w_full = sb("w_full", [P, NT])
        eps_col = sb("eps_col", [P, 1])
        silu_e = sb("silu_e", [P, B])
        silu = sb("silu", [P, B])
        mods = sb("mods", [P, 6 * B])
        neg_g = sb("neg_g", [P, 6 * B])
        sign_g = sb("sign_g", [P, 6 * B])
        gates = sb("gates", [P, 6 * B])
        bias_t = sb("bias_t", [P, 3])
        bias_0 = sb("bias_0", [P, 3])
        c2_0 = sb("c2_0", [P, 1])

        xs = sb("xs", [P, N, J * C])
        h2 = sb("h2", [P, N, NT])
        hh = sb("hh", [P, 2, T + 1])
        pp = sb("pp", [P, 2, T + 1])
        aa = sb("aa", [P, 2, T + 1])
        bb = sb("bb", [P, 2, T + 1])
        st1 = sb("st1", [P, N, J, 6])
        mv1 = sb("mv1", [P, N, J, 2])
        lv1 = sb("lv1", [P, N, J])
        nr1 = sb("nr1", [P, N, J])
        rs1 = sb("rs1", [P, N, J])
        st2 = sb("st2", [P, N, J, 6])
        mv2 = sb("mv2", [P, N, J, 2])
        lv2 = sb("lv2", [P, N, J])
        rs2 = sb("rs2", [P, N, J])
        nm2 = sb("nm2", [P, N, J])
        nr2 = sb("nr2", [P, J])
        xn1 = sb("xn1", [P, RING, J * C])
        vs = sb("vs", [P, RING, NT])
        er = sb("er", [P, RING, NT])
        f1 = sb("f1", [P, RING, NT])
        f2 = sb("f2", [P, RING, NT])
        ev = sb("ev", [P, RING, NT])
        f2v = sb("f2v", [P, RING, NT])
        den = sb("den", [P, RING, NT])
        num = sb("num", [P, RING, NT])
        xn2 = sb("xn2", [P, 2, J * C])
        tf = sb("tf", [P, CPB, NT])
        ti = sb("ti", [P, CPB, NT])
        tg = sb("tg", [P, CPB, NT])
        c2 = sb("c2", [P, CPB, NT])
        uoc = sb("uoc", [P, CPB, NT])
        pre = sb("pre", [P, RING, NT])

        banks = [ctx.enter_context(nc.psum_tensor(f"bank{i}", [P, NT], F32)) for i in range(8)]
        T1_PS, K_PS, V_PS, R_PS, WO_PS, T2_PS = banks[0], banks[1:3], banks[3], banks[4], banks[5], banks[6:8]
        MOD_PS, WOG_PS = banks[6], banks[7]
        G_PS = [banks[1:4], [banks[0], banks[4], banks[5]]]
        UOC_PS = [banks[1], banks[0]]
        FIN_PS, OT_PS = banks[2:4], banks[6:8]

        names = ("small_in att_in ffn_in ident_set minus_ident_set eps_set edges_set silu_exp silu_up silu_ready "
                 "decay_exp w_ready mod_ps mods_sb mix_ready kvr_w neg_ready gates_ready wog_ready wogT_ps wogT_ready "
                 "u_ready u_bias_ps bias_ready "
                 "stats1a stats1_ready lnvar1 rstd1_ready nr1_ready xn1_ready t1_done h_ready k_done v_done r_done "
                 "p_start p_ready d1_ready d2_ready minus_p_done f1_ready f2_ready e_ready v_ready er_ready erc_ready "
                 "b_ready f2v_ready a_ready den_ready wv_ready num_ready lr_ready ld_ready logs_ready rg_ready "
                 "y_ready wo_done x2_ready stats2a stats2_ready lnvar2 rstd2_ready nr2_ready xn2_ready t2_done h2_ready "
                 "gate_ps tf_ready ti_ready tg_ready ig_ready fc_ready c_ready uoc_ps uoc_ready fin_ps pre_ready "
                 "hf_ready hg_ready ot_done out_ready stored").split()
        S = {n: sem(n) for n in names}
        x_in = [sem(f"x_in{i}") for i in range(N)]

        def col(n):
            return cols[:, n:n + 1]

        def mod(s, b):
            return mods[:, s * B + b:s * B + b + 1]

        def gate(s, b):
            return gates[:, s * B + b:s * B + b + 1]

        def at(c):
            return (c // CPB) % 2, (c % CPB) * NT

        def after(eng, name, c, lag=0):
            if c - lag >= 0:
                eng.wait_ge(S[name], c - lag + 1)

        def pipeline(*stages):
            for tick in range(-max(lead for _, lead in stages), N - min(lead for _, lead in stages)):
                for stage, lead in stages:
                    if 0 <= tick + lead < N:
                        stage(tick + lead)

        FINALS = [(q, t) for q in range(CPB) for t in range(B)]

        block = ctx.enter_context(nc.Block())

        @block.sync
        def _(sp):
            sp.dma_start(cols[:], small).then_inc(S["small_in"], 16)
            sp.dma_start(xs[:, 0, :], x_d[:, 0, :]).then_inc(x_in[0], 16)
            sp.dma_start(w_att[:, :, :].rearrange("p n c -> p (n c)"), att_w).then_inc(S["att_in"], 16)
            for c in range(1, N):
                if c == 3:
                    sp.dma_start(w_ffn[:, :, :].rearrange("p n c -> p (n c)"), ffn_w).then_inc(S["ffn_in"], 16)
                sp.dma_start(xs[:, c, :], x_d[:, c, :]).then_inc(x_in[c], 16)
            for n, (q, t) in enumerate(FINALS):
                c = t * CPB + q
                after(sp, "out_ready", n)
                sp.dma_start(out_d[:, c, :], xs[:, c, :]).then_inc(S["stored"], 16)
            sp.wait_ge(S["stored"], 16 * N)

        @block.gpsimd
        def _(pool):
            g = nc.gpsimd
            g.memset(ident[:], 0.0).then_inc(S["ident_set"], 1)
            pool.wait_ge(S["ident_set"], 1)
            g.affine_select(out=ident[:], in_=ident[:], compare_op=ALU.not_equal, fill=1.0, base=0,
                            pattern=[[-1, P]], channel_multiplier=1).then_inc(S["ident_set"], 1)
            for tile in (hh, aa, bb):
                for k in range(2):
                    g.memset(tile[:, k, 0:1], 0.0).then_inc(S["edges_set"], 1)

            def d1(c):
                k, (m, o) = c % RING, at(c)
                after(pool, "p_ready", c)
                after(pool, "a_ready", c, RING)
                g.tensor_tensor(f1[:, k, :], pp[:, m, o:o + NT], pp[:, m, o + 1:o + 1 + NT],
                                ALU.subtract).then_inc(S["d1_ready"], 1)

            def f2v_(c):
                k = c % RING
                after(pool, "f2_ready", c)
                after(pool, "v_ready", c)
                after(pool, "a_ready", c, RING)
                g.tensor_tensor(f2v[:, k, :], f2[:, k, :], vs[:, k, :], ALU.mult).then_inc(S["f2v_ready"], 1)

            def num_(c):
                k, (m, o) = c % RING, at(c)
                after(pool, "wv_ready", c)
                after(pool, "a_ready", c)
                g.tensor_tensor(num[:, k, :], num[:, k, :], aa[:, m, o:o + NT], ALU.add).then_inc(S["num_ready"], 1)

            def logs(c):
                k = c % RING
                after(pool, "lr_ready", c)
                after(pool, "ld_ready", c)
                g.tensor_tensor(den[:, k, :], den[:, k, :], er[:, k, :], ALU.add).then_inc(S["logs_ready"], 1)

            def y(c):
                k = c % RING
                after(pool, "num_ready", c)
                after(pool, "rg_ready", c)
                g.tensor_tensor(num[:, k, :], num[:, k, :], den[:, k, :], ALU.mult).then_inc(S["y_ready"], 1)

            pipeline((y, -4), (d1, -2), (logs, -3), (num_, -3), (f2v_, -2))

            for c in range(1, N):
                """(x - mean) / std of the second layer norm"""
                k = c % 2
                after(pool, "rstd2_ready", c)
                after(pool, "t2_done", c, 2)
                for j in range(J):
                    last = g.tensor_scalar(xn2[:, k, j * C:(j + 1) * C], xs[:, c, j * C:(j + 1) * C],
                                           nm2[:, c, j:j + 1], rs2[:, c, j:j + 1], ALU.add, ALU.mult)
                last.then_inc(S["xn2_ready"], 1)
            for n, (q, t) in enumerate(FINALS):
                k = n % RING
                after(pool, "hf_ready", n)
                g.tensor_scalar(pre[:, k, :], pre[:, k, :], gate(GB, t), 1.0, ALU.mult,
                                ALU.mult).then_inc(S["hg_ready"], 1)

        @block.scalar
        def _(act):
            a = nc.scalar
            a.preload_act_table_set("natural_log_exp_and_others")
            act.wait_ge(S["small_in"], 16)
            a.activation(silu_e[:], cols[:, COND:COND + B], ACT.Exp, scale=-1.0).then_inc(S["silu_exp"], 1)
            a.activation(w_col[:], col(DECAY), ACT.Exp).then_inc(S["decay_exp"], 1)
            act.wait_ge(S["eps_set"], 1)

            def rstd1(c):
                after(act, "stats1_ready", c)
                a.activation(lv1[:, c, :], mv1[:, c, :, 1], ACT.Ln, bias=eps_col[:, 0:1]).then_inc(S["lnvar1"], 1)
                after(act, "lnvar1", c)
                a.activation(rs1[:, c, :], lv1[:, c, :], ACT.Exp, scale=-0.5).then_inc(S["rstd1_ready"], 1)

            def norm1(c):
                k = c % RING
                after(act, "nr1_ready", c)
                after(act, "t1_done", c, RING)
                for j in range(J):
                    last = a.activation(xn1[:, k, j * C:(j + 1) * C], xs[:, c, j * C:(j + 1) * C], ACT.Identity,
                                        scale=rs1[:, c, j:j + 1], bias=nr1[:, c, j:j + 1])
                last.then_inc(S["xn1_ready"], 1)

            def evac_h(c):
                m, o = at(c)
                after(act, "t1_done", c)
                if c == 0:
                    act.wait_ge(S["mods_sb"], 2)
                after(act, "r_done", c, 2 * CPB)
                a.activation(hh[:, m, o + 1:o + 1 + NT].rearrange("q (p j) -> q p j", j=J),
                             T1_PS[:, :].rearrange("q (j p) -> q p j", j=J), ACT.Identity,
                             scale=mod(CA, c // CPB), bias=mod(SA, c // CPB)).then_inc(S["h_ready"], 1)

            def evac_v(c):
                k = c % RING
                after(act, "v_done", c)
                after(act, "wv_ready", c, RING)
                after(act, "f2v_ready", c, RING)
                a.copy(vs[:, k, :], V_PS[:, :]).then_inc(S["v_ready"], 1)

            def exp_r(c):
                k = c % RING
                after(act, "r_done", c)
                after(act, "logs_ready", c, RING)
                a.activation(er[:, k, :], R_PS[:, :], ACT.Exp, scale=-1.0).then_inc(S["er_ready"], 1)

            def exp_f2(c):
                k = c % RING
                after(act, "d2_ready", c)
                a.activation(f2[:, k, :], f2[:, k, :], ACT.Exp).then_inc(S["f2_ready"], 1)

            def exp_e(c):
                k = c % RING
                after(act, "minus_p_done", c)
                after(act, "den_ready", c, RING)
                after(act, "wv_ready", c, RING)
                a.activation(ev[:, k, :], K_PS[c % 2][:, :], ACT.Exp, bias=col(FIRST)).then_inc(S["e_ready"], 1)

            def exp_f1(c):
                k = c % RING
                after(act, "d1_ready", c)
                if c == 0:
                    act.wait_ge(S["w_ready"], 1)
                a.activation(f1[:, k, :], f1[:, k, :], ACT.Exp, bias=w_col[:, 0:1]).then_inc(S["f1_ready"], 1)

            def ln_r(c):
                k = c % RING
                after(act, "erc_ready", c)
                a.activation(er[:, k, :], er[:, k, :], ACT.Ln, bias=1.0).then_inc(S["lr_ready"], 1)

            def ln_den(c):
                k = c % RING
                after(act, "den_ready", c)
                a.activation(den[:, k, :], den[:, k, :], ACT.Ln).then_inc(S["ld_ready"], 1)

            def norm2_first():
                act.wait_ge(S["nr2_ready"], 1)
                for j in range(J):
                    last = a.activation(xn2[:, 0, j * C:(j + 1) * C], xs[:, 0, j * C:(j + 1) * C], ACT.Identity,
                                        scale=rs2[:, 0, j:j + 1], bias=nr2[:, j:j + 1])
                last.then_inc(S["xn2_ready"], 1)

            def exp_rg(c):
                k = c % RING
                if c == N - 1:
                    norm2_first()
                after(act, "logs_ready", c)
                a.activation(den[:, k, :], den[:, k, :], ACT.Exp, scale=-1.0).then_inc(S["rg_ready"], 1)
                if c == N - 1:
                    evac_h2(0)

            def evac_h2(c):
                after(act, "t2_done", c)
                a.activation(h2[:, c, :], T2_PS[c % 2][:, :], ACT.Identity, scale=mod(CB, c // CPB),
                             bias=mod(SB, c // CPB)).then_inc(S["h2_ready"], 1)

            def rstd2(c):
                after(act, "stats2_ready", c)
                a.activation(lv2[:, c, :], mv2[:, c, :, 1], ACT.Ln, bias=eps_col[:, 0:1]).then_inc(S["lnvar2"], 1)
                a.mul(nm2[:, c, :], mv2[:, c, :, 0], -1.0)
                after(act, "lnvar2", c)
                a.activation(rs2[:, c, :], lv2[:, c, :], ACT.Exp, scale=-0.5).then_inc(S["rstd2_ready"], 1)

            pipeline((exp_f1, -2), (rstd1, 0), (exp_r, -2), (exp_rg, -3), (exp_e, -2), (norm1, 0), (ln_r, -2),
                     (ln_den, -2), (rstd2, -6), (evac_v, -1), (evac_h, 0), (exp_f2, -1))

            def gate_tanhs(n):
                q = n % CPB
                bias = bias_t if n >= CPB else bias_0
                if n == 0:
                    act.wait_ge(S["bias_ready"], 3)
                act.wait_ge(S["gate_ps"], 3 * n + 1)
                after(act, "c_ready", n, CPB)
                a.activation(tf[:, q, :], G_PS[q][0][:, :], ACT.Tanh, scale=0.5,
                             bias=bias[:, 0:1]).then_inc(S["tf_ready"], 1)
                act.wait_ge(S["gate_ps"], 3 * n + 2)
                a.activation(ti[:, q, :], G_PS[q][1][:, :], ACT.Tanh, scale=0.5,
                             bias=bias[:, 1:2]).then_inc(S["ti_ready"], 1)
                act.wait_ge(S["gate_ps"], 3 * n + 3)
                a.activation(tg[:, q, :], G_PS[q][2][:, :], ACT.Tanh,
                             bias=bias[:, 2:3]).then_inc(S["tg_ready"], 1)

            def evac_uoc(q):
                after(act, "uoc_ps", q)
                a.activation(uoc[:, q, :], UOC_PS[q][:, :], ACT.Identity, bias=col(BO)).then_inc(S["uoc_ready"], 1)

            def final_tanh(n):
                k = n % RING
                after(act, "pre_ready", n)
                a.activation(pre[:, k, :], pre[:, k, :], ACT.Tanh).then_inc(S["hf_ready"], 1)

            for n in range(N - 1):
                evac_h2(n + 1)
                gate_tanhs(n)
            evac_uoc(0)
            final_tanh(0)
            final_tanh(1)
            gate_tanhs(N - 1)
            for n in range(2, N):
                if n == B:
                    evac_uoc(1)
                final_tanh(n)

        @block.vector
        def _(dve):
            v = nc.vector
            v.memset(eps_col[:], EPS).then_inc(S["eps_set"], 1)
            v.memset(w_full[:], 0.0).then_inc(S["eps_set"], 1)

            dve.wait_ge(S["silu_exp"], 1)
            v.tensor_scalar(silu_e[:], silu_e[:], 1.0, None, ALU.add).then_inc(S["silu_up"], 1)
            dve.wait_ge(S["silu_up"], 1)
            v.reciprocal(silu_e[:], silu_e[:]).then_inc(S["silu_up"], 1)
            dve.wait_ge(S["silu_up"], 2)
            v.tensor_tensor(silu[:], silu_e[:], cols[:, COND:COND + B], ALU.mult).then_inc(S["silu_ready"], 1)

            def weights_and_modulation():
                v.tensor_scalar(one_minus[:], cols[:, MIXK:MIXR + 1], -1.0, 1.0, ALU.mult,
                                ALU.add).then_inc(S["mix_ready"], 1)
                dve.wait_ge(S["decay_exp"], 1)
                v.tensor_scalar(w_col[:], w_col[:], -1.0, None, ALU.mult).then_inc(S["w_ready"], 1)
                dve.wait_ge(S["w_ready"], 1)
                dve.wait_ge(S["eps_set"], 2)
                v.tensor_scalar(w_full[:], w_full[:], w_col[:, 0:1], None, ALU.add).then_inc(S["w_ready"], 1)
                dve.wait_ge(S["ident_set"], 2)
                v.tensor_scalar(minus_ident[:], ident[:], -1.0, None, ALU.mult).then_inc(S["minus_ident_set"], 1)
                dve.wait_ge(S["att_in"], 16)
                dve.wait_ge(S["mix_ready"], 1)
                for n in range(3):
                    v.tensor_scalar(w_now[:, n, :], w_att[:, WK + n, :], col(MIXK + n), None, ALU.mult)
                    v.tensor_scalar(w_prev[:, n, :], w_att[:, WK + n, :], one_minus[:, n:n + 1], None,
                                    ALU.mult).then_inc(S["kvr_w"], 1)
                dve.wait_ge(S["mod_ps"], 1)
                v.tensor_copy(mods[:], MOD_PS[:, 0:6 * B]).then_inc(S["mods_sb"], 1)
                dve.wait_ge(S["mods_sb"], 1)
                scales = mods[:, :].rearrange("p (h s b) -> p h s b", h=2, s=3)[:, :, CA, :]
                v.tensor_scalar(scales, scales, 1.0, None, ALU.add).then_inc(S["mods_sb"], 1)

            def gated_wo():
                v.tensor_scalar(neg_g[:], mods[:], -1.0, None, ALU.mult).then_inc(S["neg_ready"], 1)
                v.tensor_scalar(sign_g[:], mods[:], 0.0, 2.0, ALU.is_ge, ALU.mult).then_inc(S["neg_ready"], 1)
                dve.wait_ge(S["neg_ready"], 2)
                v.scalar_tensor_tensor(out=neg_g[:], in0=neg_g[:], scalar=GATE_MIN, in1=mods[:], op0=ALU.max,
                                       op1=ALU.max).then_inc(S["neg_ready"], 1)
                dve.wait_ge(S["neg_ready"], 3)
                v.scalar_tensor_tensor(out=gates[:], in0=sign_g[:], scalar=-1.0, in1=neg_g[:], op0=ALU.add,
                                       op1=ALU.mult).then_inc(S["gates_ready"], 1)
                dve.wait_ge(S["gates_ready"], 1)
                for b in range(B):
                    last = v.tensor_scalar(wo_g[:, b, :], w_att[:, WO_ATT, :], gate(GA, b), None, ALU.mult)
                last.then_inc(S["wog_ready"], 1)

            def halved_u():
                dve.wait_ge(S["wogT_ps"], 1)
                v.tensor_copy(wo_gT[:], WOG_PS[:, :]).then_inc(S["wogT_ready"], 1)
                dve.wait_ge(S["ffn_in"], 16)
                v.tensor_scalar(u_half[:, :, :], w_ffn[:, UF:UF + 4, :], 0.5, None, ALU.mult).then_inc(S["u_ready"], 1)
                v.tensor_scalar(c2_0[:], col(INC), 2.0, None, ALU.mult).then_inc(S["u_ready"], 1)
                v.tensor_scalar(bias_t[:, 0:2], cols[:, BF:BI + 1], 0.5, None, ALU.mult)
                v.tensor_copy(bias_t[:, 2:3], col(BC)).then_inc(S["bias_ready"], 1)

            def first_biases():
                dve.wait_ge(S["u_bias_ps"], 1)
                dve.wait_ge(S["bias_ready"], 1)
                v.scalar_tensor_tensor(out=bias_0[:, 0:2], in0=MOD_PS[:, 0:2], scalar=0.5, in1=bias_t[:, 0:2],
                                       op0=ALU.mult, op1=ALU.add).then_inc(S["bias_ready"], 1)
                v.tensor_tensor(bias_0[:, 2:3], MOD_PS[:, 2:3], bias_t[:, 2:3], ALU.add).then_inc(S["bias_ready"], 1)

            later_setup = {1: gated_wo, 2: halved_u, 3: first_biases}

            def token_stats(c, st, mv, part, ready):
                for j in range(J):
                    last = v.bn_stats(st[:, c, j, :], xs[:, c, j * C:(j + 1) * C])
                last.then_inc(S[part], 1)
                after(dve, part, c)
                for j in range(J):
                    last = v.bn_aggr(mv[:, c, j, :], st[:, c, j, :])
                last.then_inc(S[ready], 1)

            def stats1(c):
                dve.wait_ge(x_in[c], 16)
                token_stats(c, st1, mv1, "stats1a", "stats1_ready")

            def minus_mean1(c):
                after(dve, "rstd1_ready", c)
                v.scalar_tensor_tensor(out=nr1[:, c, :], in0=mv1[:, c, :, 0], scalar=-1.0, in1=rs1[:, c, :],
                                       op0=ALU.mult, op1=ALU.mult).then_inc(S["nr1_ready"], 1)
                if c == 0:
                    weights_and_modulation()

            def run_max(c):
                k, (m, o) = c % 2, at(c)
                if c in later_setup:
                    later_setup[c]()
                after(dve, "k_done", c)
                if c == 0:
                    dve.wait_ge(S["w_ready"], 2)
                    dve.wait_ge(S["edges_set"], 6)
                after(dve, "p_ready", c, 1)
                after(dve, "d1_ready", c, 2 * CPB)
                after(dve, "minus_p_done", c, 2 * CPB)
                if c % CPB == 0:
                    v.tensor_copy(pp[:, m, 0:1], K_PS[k][:, 0:1]).then_inc(S["p_start"], 1)
                    dve.wait_ge(S["p_start"], c // CPB + 1)
                v.tensor_tensor_scan(pp[:, m, o + 1:o + 1 + NT], w_full[:], K_PS[k][:, :], pp[:, m, o:o + 1],
                                     ALU.add, ALU.max).then_inc(S["p_ready"], 1)

            def d2(c):
                k, (m, o) = c % RING, at(c)
                after(dve, "p_ready", c)
                after(dve, "f2v_ready", c, RING)
                v.tensor_tensor(f2[:, k, :], K_PS[c % 2][:, :], pp[:, m, o + 1:o + 1 + NT],
                                ALU.subtract).then_inc(S["d2_ready"], 1)

            def cap_r(c):
                k = c % RING
                after(dve, "er_ready", c)
                v.tensor_scalar(er[:, k, :], er[:, k, :], CAP, None, ALU.min).then_inc(S["erc_ready"], 1)

            def scan_b(c):
                k, (m, o) = c % RING, at(c)
                after(dve, "f1_ready", c)
                after(dve, "f2_ready", c)
                after(dve, "b_ready", c, 1)
                v.tensor_tensor_scan(bb[:, m, o + 1:o + 1 + NT], f1[:, k, :], f2[:, k, :], bb[:, m, o:o + 1],
                                     ALU.mult, ALU.add).then_inc(S["b_ready"], 1)

            def scan_a(c):
                k, (m, o) = c % RING, at(c)
                after(dve, "f1_ready", c)
                after(dve, "f2v_ready", c)
                after(dve, "a_ready", c, 1)
                after(dve, "num_ready", c, 2 * CPB)
                v.tensor_tensor_scan(aa[:, m, o + 1:o + 1 + NT], f1[:, k, :], f2v[:, k, :], aa[:, m, o:o + 1],
                                     ALU.mult, ALU.add).then_inc(S["a_ready"], 1)

            def weigh_v(c):
                k = c % RING
                after(dve, "e_ready", c)
                after(dve, "v_ready", c)
                after(dve, "wo_done", c, RING)
                v.scalar_tensor_tensor(out=num[:, k, :], in0=ev[:, k, :], scalar=CAP, in1=vs[:, k, :],
                                       op0=ALU.min, op1=ALU.mult).then_inc(S["wv_ready"], 1)

            def den_(c):
                k, (m, o) = c % RING, at(c)
                after(dve, "e_ready", c)
                after(dve, "b_ready", c)
                after(dve, "y_ready", c, RING)
                v.scalar_tensor_tensor(out=den[:, k, :], in0=ev[:, k, :], scalar=CAP, in1=bb[:, m, o:o + NT],
                                       op0=ALU.min, op1=ALU.add).then_inc(S["den_ready"], 1)

            def residual(c):
                after(dve, "wo_done", c)
                v.tensor_tensor(xs[:, c, :], WO_PS[:, :], xs[:, c, :], ALU.add).then_inc(S["x2_ready"], 1)

            def stats2(c):
                after(dve, "x2_ready", c)
                token_stats(c, st2, mv2, "stats2a", "stats2_ready")
                if c == N // 2:
                    dve.wait_ge(S["rstd2_ready"], 1)
                    v.scalar_tensor_tensor(out=nr2[:], in0=mv2[:, 0, :, 0], scalar=-1.0, in1=rs2[:, 0, :],
                                           op0=ALU.mult, op1=ALU.mult).then_inc(S["nr2_ready"], 1)

            pipeline((stats1, 0), (scan_a, -3), (stats2, -5), (minus_mean1, 0), (scan_b, -2), (cap_r, -2), (run_max,
                     -1), (den_, -2), (residual, -4), (d2, -1), (weigh_v, -2))

            def state(n):
                q = n % CPB
                after(dve, "tf_ready", n)
                if n >= CPB:
                    after(dve, "c_ready", n, CPB)
                    v.scalar_tensor_tensor(out=tf[:, q, :], in0=tf[:, q, :], scalar=1.0, in1=c2[:, q, :],
                                           op0=ALU.add, op1=ALU.mult).then_inc(S["fc_ready"], 1)
                else:
                    dve.wait_ge(S["u_ready"], 2)
                    v.tensor_scalar(tf[:, q, :], tf[:, q, :], 1.0, c2_0[:, 0:1], ALU.add,
                                    ALU.mult).then_inc(S["fc_ready"], 1)
                after(dve, "ti_ready", n)
                after(dve, "tg_ready", n)
                v.scalar_tensor_tensor(out=ti[:, q, :], in0=ti[:, q, :], scalar=1.0, in1=tg[:, q, :],
                                       op0=ALU.add, op1=ALU.mult).then_inc(S["ig_ready"], 1)
                after(dve, "fc_ready", n)
                after(dve, "ig_ready", n)
                v.scalar_tensor_tensor(out=c2[:, q, :], in0=tf[:, q, :], scalar=0.5, in1=ti[:, q, :],
                                       op0=ALU.mult, op1=ALU.add).then_inc(S["c_ready"], 1)

            def before_tanh(n):
                q, _ = FINALS[n]
                k = n % RING
                after(dve, "fin_ps", n)
                after(dve, "uoc_ready", q)
                after(dve, "ot_done", n, RING)
                v.tensor_tensor(pre[:, k, :], FIN_PS[n % 2][:, :], uoc[:, q, :], ALU.add).then_inc(S["pre_ready"], 1)

            def output(n):
                q, t = FINALS[n]
                c = t * CPB + q
                after(dve, "ot_done", n)
                v.tensor_tensor(xs[:, c, :], OT_PS[n % 2][:, :], xs[:, c, :], ALU.add).then_inc(S["out_ready"], 1)

            for n in range(N - 1):
                state(n)
            before_tanh(0)
            before_tanh(1)
            state(N - 1)
            for n in range(2, N + 2):
                if n < N:
                    before_tanh(n)
                output(n - 2)

        @block.tensor
        def _(pe):
            t_ = nc.tensor
            pe.wait_ge(S["ident_set"], 2)
            for _ in range(WARM_UP):
                t_.matmul(MOD_PS[:, 0:P], ident[:, :], ident[:, :], start=True, stop=True)
            pe.wait_ge(S["att_in"], 16)
            pe.wait_ge(S["silu_ready"], 1)
            for s in range(6):
                last = t_.matmul(MOD_PS[:, s * B:(s + 1) * B], w_att[:, WMOD + s, :], silu[:], start=True, stop=True)
            last.then_inc(S["mod_ps"], 1)

            def turn1(c):
                k = c % RING
                after(pe, "xn1_ready", c)
                after(pe, "h_ready", c, 1)
                if c == 0:
                    pe.wait_ge(S["ident_set"], 2)
                for j in range(J):
                    last = t_.transpose(T1_PS[:, j * P:(j + 1) * P], xn1[:, k, j * C:(j + 1) * C], ident[:, :])
                last.then_inc(S["t1_done"], 1)

            def project(c, n, bank, done):
                m, o = at(c)
                after(pe, "h_ready", c)
                if c == 0:
                    pe.wait_ge(S["kvr_w"], n + 1)
                    pe.wait_ge(S["edges_set"], 6)
                t_.matmul(bank[:, :], w_now[:, n, :], hh[:, m, o + 1:o + 1 + NT], start=True, stop=False)
                t_.matmul(bank[:, :], w_prev[:, n, :], hh[:, m, o:o + NT], start=False,
                          stop=True).then_inc(S[done], 1)

            def project_k(c):
                after(pe, "e_ready", c, 2)
                project(c, 0, K_PS[c % 2], "k_done")

            def project_v(c):
                after(pe, "v_ready", c, 1)
                project(c, 1, V_PS, "v_done")

            def project_r(c):
                after(pe, "er_ready", c, 1)
                project(c, 2, R_PS, "r_done")

            def minus_p(c):
                m, o = at(c)
                after(pe, "d2_ready", c)
                if c == 0:
                    pe.wait_ge(S["minus_ident_set"], 1)
                t_.matmul(K_PS[c % 2][:, :], minus_ident[:, :], pp[:, m, o:o + NT], start=False, stop=True,
                          skip_group_check=True).then_inc(S["minus_p_done"], 1)
                if c == 1:
                    pe.wait_ge(S["wog_ready"], 1)
                    for b in range(B):
                        last = t_.transpose(WOG_PS[:, b * C:(b + 1) * C], wo_g[:, b, :], ident[:, :])
                    last.then_inc(S["wogT_ps"], 1)
                if c == 2:
                    pe.wait_ge(S["u_ready"], 2)
                    for n in range(3):
                        last = t_.matmul(MOD_PS[:, n:n + 1], u_half[:, n, :], c2_0[:], start=True, stop=True)
                    last.then_inc(S["u_bias_ps"], 1)

            def turn2(c):
                after(pe, "xn2_ready", c)
                after(pe, "h2_ready", c, 2)
                if c == 0:
                    pe.wait_ge(S["bias_ready"], 3)
                for j in range(J):
                    last = t_.transpose(T2_PS[c % 2][:, j * P:(j + 1) * P], xn2[:, c % 2, j * C:(j + 1) * C],
                                        ident[:, :])
                last.then_inc(S["t2_done"], 1)

            def keep_clock(products):
                pe.wait_ge(S["h_ready"], N)
                for _ in range(products):
                    t_.matmul(T1_PS[:, 0:P], ident[:, :], ident[:, :], start=True, stop=True)

            def project_out(c):
                k = c % RING
                if c >= N - 2:
                    keep_clock(16)
                if c == N - 1:
                    turn2(0)
                after(pe, "y_ready", c)
                if c == 0:
                    pe.wait_ge(S["wogT_ready"], 1)
                after(pe, "x2_ready", c, 1)
                y = num[:, k, :].rearrange("q (p j) -> q j p", j=J)
                b = c // CPB
                for j in range(J):
                    last = t_.matmul(WO_PS[:, j * C:(j + 1) * C], y[:, j, :], wo_gT[:, b * C:(b + 1) * C],
                                     start=True, stop=True)
                last.then_inc(S["wo_done"], 1)

            pipeline((project_out, -4), (project_v, -1), (turn1, 0), (project_r, -1), (minus_p, -1), (project_k, 0))

            def gates_x(n):
                q = n % CPB
                after(pe, "h2_ready", n)
                for w, read in enumerate(("tf_ready", "ti_ready", "tg_ready")):
                    after(pe, read, n, CPB)
                    if n == CPB - 1 and w == 2:
                        after(pe, "x2_ready", N - 1)
                    last = t_.matmul(G_PS[q][w][:, :], w_ffn[:, WF + w, :], h2[:, n, :], start=True, stop=(n < CPB))
                    if n < CPB:
                        last.then_inc(S["gate_ps"], 1)
                    if w == 1 and n + 1 < N:
                        turn2(n + 1)

            def gates_c(n):
                q = n % CPB
                after(pe, "c_ready", n, CPB)
                for w in range(3):
                    t_.matmul(G_PS[q][w][:, :], u_half[:, w, :], c2[:, q, :], start=False,
                              stop=True).then_inc(S["gate_ps"], 1)

            def final_c(q):
                after(pe, "c_ready", N - CPB + q)
                t_.matmul(UOC_PS[q][:, :], u_half[:, 3, :], c2[:, q, :], start=True, stop=True).then_inc(S["uoc_ps"], 1)

            def final_x(n):
                q, t = FINALS[n]
                after(pe, "pre_ready", n, 2)
                t_.matmul(FIN_PS[n % 2][:, :], w_ffn[:, WO_FFN, :], h2[:, t * CPB + q, :], start=True,
                          stop=True).then_inc(S["fin_ps"], 1)

            def turn_back(n):
                k = n % RING
                after(pe, "hg_ready", n)
                after(pe, "out_ready", n, 2)
                for j in range(J):
                    last = t_.transpose(OT_PS[n % 2][:, j * C:(j + 1) * C], pre[:, k, j * P:(j + 1) * P], ident[:, :])
                last.then_inc(S["ot_done"], 1)

            for n in range(N):
                gates_x(n)
                if n + 1 == N:
                    final_c(0)
                    final_x(0)
                    final_x(1)
                if n >= CPB:
                    gates_c(n)
            for n in range(2, N + 2):
                if n < N:
                    final_x(n)
                turn_back(n - 2)
                if n == B:
                    final_c(1)


def kernel(**inputs):
    import numpy as _np
    import concourse.bacc as _bacc
    from concourse import mybir as _mybir
    from concourse.bass_utils import run_bass_kernel_spmd as _run

    a = {name: _np.asarray(v) for name, v in inputs.items()}
    x = _np.ascontiguousarray(a["L0_attn_x"])
    columns = [a[f"L0_attn_{n}"].reshape(-1) for n in ("time_decay", "time_first", "time_mix_k", "time_mix_v",
                                                       "time_mix_r")]
    columns += [a[f"L0_ffn_{n}"] for n in ("bf", "bi", "bc", "bo", "in_c")]
    arrays = {
        "x": x,
        "small": _np.stack([*columns, *a["L0_c"]], axis=1),
        "att_w": _np.concatenate([a["L0_attn_Wk"].T, a["L0_attn_Wv"].T, a["L0_attn_Wr"].T, a["L0_attn_Wo"],
                                  a["L0_wmod"]], axis=1),
        "ffn_w": _np.concatenate([a[f"L0_ffn_{n}"].T for n in ("wf", "wi", "wc", "wo", "uf", "ui", "uc", "uo")],
                                 axis=1),
    }
    nc = _bacc.Bacc("TRN2", target_bir_lowering=False, num_devices=1)
    args = [nc.dram_tensor(n, v.shape, _mybir.dt.from_np(v.dtype), kind="ExternalInput").ap()
            for n, v in arrays.items()]
    args.append(nc.dram_tensor("out_0", x.shape, F32, kind="ExternalOutput").ap())
    adaln_rwkv_block_kernel(nc, *args)
    r = _run(nc, [arrays], core_ids=[0])
    return r.results[0]["out_0"]
```

```python
from contextlib import ExitStack

import concourse.bass as bass
from concourse import mybir

F32 = mybir.dt.float32
F32R = mybir.dt.float32r
I32 = mybir.dt.int32
ALU = mybir.AluOpType
ACT = mybir.ActivationFunctionType

C = 128
P = 128
NT = 512
J = NT // P
EPS = 1e-5
CAP = float(2 ** 62)
GATE_MIN = 0.25
WARM_UP = 11
NEWTON = 3
SHARED = 2
RING = 3

DECAY, FIRST, MIXK, MIXV, MIXR, BF, BI, BC, BO, INC, COND = range(11)
SA, CA, GA, SB, CB, GB = range(6)


WK, WV, WR, WO_ATT, WMOD = range(5)
WF, WI, WC, WO_FFN, UF, UI, UC, UO_FFN = range(8)


def adaln_rwkv_block_kernel(nc, x, small, att_w, ffn_w, out):
    B, T, _ = x.shape
    CPB = T // NT
    N = B * CPB

    x_d = x.rearrange("b (c p j) d -> p (b c) (j d)", c=CPB, j=J)
    out_d = out.rearrange("b (c p j) d -> p (b c) (j d)", c=CPB, j=J)

    with ExitStack() as ctx:
        def sb(name, shape, dtype=F32):
            return ctx.enter_context(nc.sbuf_tensor(name, shape, dtype))

        def sem(name):
            return ctx.enter_context(nc.semaphore(name))

        ident = sb("ident", [P, P])
        minus_ident = sb("minus_ident", [P, P])
        cols = sb("cols", [P, COND + B])
        w_att = sb("w_att", [P, 10, C])
        w_ffn = sb("w_ffn", [P, 8, C])
        w_hi = sb("w_hi", [P, 8, C], F32R)
        w_lo = sb("w_lo", [P, 8, C], F32R)
        w_now = sb("w_now", [P, 3, C])
        w_prev = sb("w_prev", [P, 3, C])
        wo_g = sb("wo_g", [P, B, C])
        wo_gT = sb("wo_gT", [P, B * C])
        one_minus = sb("one_minus", [P, 3])
        w_col = sb("w_col", [P, 1])
        w_full = sb("w_full", [P, NT])
        eps_col = sb("eps_col", [P, 1])
        silu_e = sb("silu_e", [P, B])
        silu = sb("silu", [P, B])
        mods = sb("mods", [P, 6 * B])
        neg_g = sb("neg_g", [P, 6 * B])
        sign_g = sb("sign_g", [P, 6 * B])
        gates = sb("gates", [P, 6 * B])
        bias_t = sb("bias_t", [P, 3])
        bias_0 = sb("bias_0", [P, 3])
        c2_0 = sb("c2_0", [P, 1])

        xs = sb("xs", [P, N, J * C])
        h2 = sb("h2", [P, 2, NT])
        h2_hi = sb("h2_hi", [P, N, NT], F32R)
        h2_lo = sb("h2_lo", [P, N, NT], F32R)
        hh = sb("hh", [P, 2, T + 1])
        pp = sb("pp", [P, 2, T + 1])
        aa = sb("aa", [P, 2, T + 1])
        bb = sb("bb", [P, 2, T + 1])
        st1 = sb("st1", [P, N, J, 6])
        mv1 = sb("mv1", [P, N, J, 2])
        lv1 = sb("lv1", [P, N, J])
        nr1 = sb("nr1", [P, N, J])
        rs1 = sb("rs1", [P, N, J])
        st2 = sb("st2", [P, N, J, 6])
        mv2 = sb("mv2", [P, N, J, 2])
        lv2 = sb("lv2", [P, N, J])
        rs2 = sb("rs2", [P, N, J])
        nm2 = sb("nm2", [P, N, J])
        var_l = sb("var_l", [P, N // 2 - 1, J])
        bits_l = sb("bits_l", [P, N // 2 - 1, J], I32)
        guess_l = sb("guess_l", [P, N // 2 - 1, J])
        y2_l = sb("y2_l", [P, N // 2 - 1, J])
        xn1 = sb("xn1", [P, RING, J * C])
        vs = sb("vs", [P, RING, NT])
        er = sb("er", [P, RING, NT])
        f1 = sb("f1", [P, RING, NT])
        f2 = sb("f2", [P, RING, NT])
        ev = sb("ev", [P, RING, NT])
        f2v = sb("f2v", [P, RING, NT])
        den = sb("den", [P, RING, NT])
        num = sb("num", [P, RING, NT])
        xn2 = sb("xn2", [P, 2, J * C])
        tf = sb("tf", [P, CPB, NT])
        ti = sb("ti", [P, CPB, NT])
        tg = sb("tg", [P, CPB, NT])
        c2 = sb("c2", [P, CPB, NT])
        c2_hi = sb("c2_hi", [P, CPB, NT], F32R)
        c2_lo = sb("c2_lo", [P, CPB, NT], F32R)
        uoc = sb("uoc", [P, NT])
        pre = sb("pre", [P, B, NT])

        banks = [ctx.enter_context(nc.psum_tensor(f"bank{i}", [P, NT], F32)) for i in range(8)]
        T1_PS, K_PS, V_PS, R_PS, WO_PS, T2_PS = banks[0], banks[1:3], banks[3], banks[4], banks[5], banks[6:8]
        MOD_PS, WOG_PS = banks[6], banks[7]
        G_PS = [banks[1:4], [banks[0], banks[4], banks[5]]]
        UOC_PS, OT_PS = banks[1], banks[6:8]
        FIN_PS = banks[2:4] + banks[6:8] + [banks[0], banks[4], banks[5], banks[1]]

        names = ("small_in mod_in att_in ffn_in ident_set minus_ident_set eps_set edges_set silu_exp silu_up "
                 "silu_ready decay_exp w_ready mod_ps mods_sb mix_ready kvr_w neg_ready gates_ready wog_ready "
                 "wogT_ps wogT_ready w_hi_ready w_lo_ready c2_0_ready u_bias_ps bias_ready stats1a stats1_ready "
                 "lnvar1 rstd1_ready nr1_ready xn1_half xn1_ready t1_done h_ready k_done v_done r_done p_start "
                 "p_ready d1_ready d2_ready minus_p_done f1_ready f2_ready e_ready v_ready er_ready erc_ready "
                 "b_ready f2v_ready a_ready den_ready wv_ready num_ready lr_ready ld_ready logs_ready rg_ready "
                 "y_ready last_logs last_num last_y wo_done x2_ready stats2a stats2_ready lnvar2 rstd2_ready "
                 "rstd2_late newton xn2_ready t2_done h2_ready h2_hi_ready h2_lo_ready gate_ps tf_ready ti_ready "
                 "tg_ready ig_ready fc_ready c_ready c_hi_ready c_lo_ready uoc_ps uoc_ready fin_ps fin2_ps "
                 "pre_ready hf_ready hg_ready ot_done out_ready stored").split()
        S = {n: sem(n) for n in names}
        x_in = [sem(f"x_in{i}") for i in range(N)]

        def col(n):
            return cols[:, n:n + 1]

        def mod(s, b):
            return mods[:, s * B + b:s * B + b + 1]

        def gate(s, b):
            return gates[:, s * B + b:s * B + b + 1]

        def at(c):
            return (c // CPB) % 2, (c % CPB) * NT

        def after(eng, name, c, lag=0):
            if c - lag >= 0:
                eng.wait_ge(S[name], c - lag + 1)

        def pipeline(*stages, ends={}):
            for tick in range(-max(lead for _, lead in stages), N - min(lead for _, lead in stages)):
                for stage, lead in stages:
                    if 0 <= tick + lead < ends.get(stage.__name__, N):
                        stage(tick + lead)

        FINALS = [(q, t) for q in range(CPB) for t in range(B)]

        block = ctx.enter_context(nc.Block())

        @block.sync
        def _(sp):
            sp.dma_start(cols[:], small).then_inc(S["small_in"], 16)
            sp.dma_start(xs[:, 0, :], x_d[:, 0, :]).then_inc(x_in[0], 16)
            sp.dma_start(w_att[:, WMOD:, :].rearrange("p n c -> p (n c)"), att_w[:, WMOD * C:]).then_inc(S["mod_in"], 16)
            sp.dma_start(w_att[:, :WMOD, :].rearrange("p n c -> p (n c)"), att_w[:, :WMOD * C]).then_inc(S["att_in"], 16)
            for c in range(1, N):
                if c == 3:
                    sp.dma_start(w_ffn[:, :, :].rearrange("p n c -> p (n c)"), ffn_w).then_inc(S["ffn_in"], 16)
                sp.dma_start(xs[:, c, :], x_d[:, c, :]).then_inc(x_in[c], 16)
            for n, (q, t) in enumerate(FINALS):
                c = t * CPB + q
                after(sp, "out_ready", n)
                sp.dma_start(out_d[:, c, :], xs[:, c, :]).then_inc(S["stored"], 16)
            sp.wait_ge(S["stored"], 16 * N)

        @block.gpsimd
        def _(pool):
            g = nc.gpsimd
            g.memset(ident[:], 0.0).then_inc(S["ident_set"], 1)
            pool.wait_ge(S["ident_set"], 1)
            g.affine_select(out=ident[:], in_=ident[:], compare_op=ALU.not_equal, fill=1.0, base=0,
                            pattern=[[-1, P]], channel_multiplier=1).then_inc(S["ident_set"], 1)
            for tile in (hh, aa, bb):
                for k in range(2):
                    g.memset(tile[:, k, 0:1], 0.0).then_inc(S["edges_set"], 1)

            def d1(c):
                k, (m, o) = c % RING, at(c)
                after(pool, "p_ready", c)
                after(pool, "a_ready", c, RING)
                g.tensor_tensor(f1[:, k, :], pp[:, m, o:o + NT], pp[:, m, o + 1:o + 1 + NT],
                                ALU.subtract).then_inc(S["d1_ready"], 1)

            def f2v_(c):
                k = c % RING
                after(pool, "f2_ready", c)
                after(pool, "v_ready", c)
                after(pool, "a_ready", c, RING)
                g.tensor_tensor(f2v[:, k, :], f2[:, k, :], vs[:, k, :], ALU.mult).then_inc(S["f2v_ready"], 1)

            def num_(c):
                k, (m, o) = c % RING, at(c)
                after(pool, "wv_ready", c)
                after(pool, "a_ready", c)
                g.tensor_tensor(num[:, k, :], num[:, k, :], aa[:, m, o:o + NT], ALU.add).then_inc(S["num_ready"], 1)

            def logs(c):
                k = c % RING
                after(pool, "lr_ready", c)
                after(pool, "ld_ready", c)
                g.tensor_tensor(den[:, k, :], den[:, k, :], er[:, k, :], ALU.add).then_inc(S["logs_ready"], 1)

            def y(c):
                k = c % RING
                after(pool, "num_ready", c)
                after(pool, "rg_ready", c)
                g.tensor_tensor(num[:, k, :], num[:, k, :], den[:, k, :], ALU.mult).then_inc(S["y_ready"], 1)

            pipeline((y, -4), (d1, -2), (logs, -3), (num_, -3), (f2v_, -2),
                     ends=dict(num_=N - 1, logs=N - 1, y=N - 1))

            def h2_low(c):
                after(pool, "h2_ready", c)
                after(pool, "h2_hi_ready", c)
                g.tensor_tensor(h2_lo[:, c, :], h2[:, c % 2, :], h2_hi[:, c, :].bitcast(F32),
                                ALU.subtract).then_inc(S["h2_lo_ready"], 1)

            def norm2(c):
                k = c % 2
                if c <= N // 2:
                    after(pool, "rstd2_ready", c)
                else:
                    pool.wait_ge(S["rstd2_late"], 1)
                after(pool, "t2_done", c, 2)
                for j in range(J):
                    last = g.tensor_scalar(xn2[:, k, j * C:(j + 1) * C], xs[:, c, j * C:(j + 1) * C],
                                           nm2[:, c, j:j + 1], rs2[:, c, j:j + 1], ALU.add, ALU.mult)
                last.then_inc(S["xn2_ready"], 1)

            norm2(0)
            for c in range(1, N):
                norm2(c)
                h2_low(c - 1)
            h2_low(N - 1)
            for n, (q, t) in enumerate(FINALS):
                k = n % B
                after(pool, "hf_ready", n)
                g.tensor_scalar(pre[:, k, :], pre[:, k, :], gate(GB, t), 1.0, ALU.mult,
                                ALU.mult).then_inc(S["hg_ready"], 1)

        @block.scalar
        def _(act):
            a = nc.scalar
            a.preload_act_table_set("natural_log_exp_and_others")
            act.wait_ge(S["small_in"], 16)
            a.activation(silu_e[:], cols[:, COND:COND + B], ACT.Exp, scale=-1.0).then_inc(S["silu_exp"], 1)
            a.activation(w_col[:], col(DECAY), ACT.Exp).then_inc(S["decay_exp"], 1)
            act.wait_ge(S["eps_set"], 1)

            def rstd1(c):
                after(act, "stats1_ready", c)
                a.activation(lv1[:, c, :], mv1[:, c, :, 1], ACT.Ln, bias=eps_col[:, 0:1]).then_inc(S["lnvar1"], 1)
                after(act, "lnvar1", c)
                a.activation(rs1[:, c, :], lv1[:, c, :], ACT.Exp, scale=-0.5).then_inc(S["rstd1_ready"], 1)

            def norm1(c):
                k = c % RING
                after(act, "nr1_ready", c)
                after(act, "t1_done", c, RING)
                for j in range(J // 2 if c < SHARED else J):
                    last = a.activation(xn1[:, k, j * C:(j + 1) * C], xs[:, c, j * C:(j + 1) * C], ACT.Identity,
                                        scale=rs1[:, c, j:j + 1], bias=nr1[:, c, j:j + 1])
                last.then_inc(S["xn1_ready"], 1)

            def evac_h(c):
                m, o = at(c)
                after(act, "t1_done", c)
                if c == 0:
                    act.wait_ge(S["mods_sb"], 2)
                after(act, "r_done", c, 2 * CPB)
                a.activation(hh[:, m, o + 1:o + 1 + NT].rearrange("q (p j) -> q p j", j=J),
                             T1_PS[:, :].rearrange("q (j p) -> q p j", j=J), ACT.Identity,
                             scale=mod(CA, c // CPB), bias=mod(SA, c // CPB)).then_inc(S["h_ready"], 1)

            def evac_v(c):
                k = c % RING
                after(act, "v_done", c)
                after(act, "wv_ready", c, RING)
                after(act, "f2v_ready", c, RING)
                a.copy(vs[:, k, :], V_PS[:, :]).then_inc(S["v_ready"], 1)

            def exp_r(c):
                k = c % RING
                after(act, "r_done", c)
                after(act, "logs_ready", c, RING)
                a.activation(er[:, k, :], R_PS[:, :], ACT.Exp, scale=-1.0).then_inc(S["er_ready"], 1)

            def exp_f2(c):
                k = c % RING
                after(act, "d2_ready", c)
                a.activation(f2[:, k, :], f2[:, k, :], ACT.Exp).then_inc(S["f2_ready"], 1)

            def exp_e(c):
                k = c % RING
                after(act, "minus_p_done", c)
                after(act, "den_ready", c, RING)
                after(act, "wv_ready", c, RING)
                a.activation(ev[:, k, :], K_PS[c % 2][:, :], ACT.Exp, bias=col(FIRST)).then_inc(S["e_ready"], 1)

            def exp_f1(c):
                k = c % RING
                after(act, "d1_ready", c)
                if c == 0:
                    act.wait_ge(S["w_ready"], 1)
                a.activation(f1[:, k, :], f1[:, k, :], ACT.Exp, bias=w_col[:, 0:1]).then_inc(S["f1_ready"], 1)

            def ln_r(c):
                k = c % RING
                after(act, "erc_ready", c)
                a.activation(er[:, k, :], er[:, k, :], ACT.Ln, bias=1.0).then_inc(S["lr_ready"], 1)

            def ln_den(c):
                k = c % RING
                after(act, "den_ready", c)
                a.activation(den[:, k, :], den[:, k, :], ACT.Ln).then_inc(S["ld_ready"], 1)

            def exp_rg(c):
                k = c % RING
                if c < N - 1:
                    after(act, "logs_ready", c)
                else:
                    act.wait_ge(S["last_logs"], 1)
                a.activation(den[:, k, :], den[:, k, :], ACT.Exp, scale=-1.0).then_inc(S["rg_ready"], 1)

            def evac_h2_hi(c):
                after(act, "t2_done", c)
                a.activation(h2_hi[:, c, :], T2_PS[c % 2][:, :], ACT.Identity, scale=mod(CB, c // CPB),
                             bias=mod(SB, c // CPB)).then_inc(S["h2_hi_ready"], 1)

            def evac_h2(c):
                after(act, "t2_done", c)
                after(act, "h2_lo_ready", c, 2)
                a.activation(h2[:, c % 2, :], T2_PS[c % 2][:, :], ACT.Identity, scale=mod(CB, c // CPB),
                             bias=mod(SB, c // CPB)).then_inc(S["h2_ready"], 1)

            def rstd2(c):
                after(act, "stats2_ready", c)
                a.activation(lv2[:, c, :], mv2[:, c, :, 1], ACT.Ln, bias=eps_col[:, 0:1]).then_inc(S["lnvar2"], 1)
                a.mul(nm2[:, c, :], mv2[:, c, :, 0], -1.0)
                after(act, "lnvar2", c)
                a.activation(rs2[:, c, :], lv2[:, c, :], ACT.Exp, scale=-0.5).then_inc(S["rstd2_ready"], 1)

            pipeline((exp_f1, -2), (rstd1, 0), (exp_r, -2), (exp_rg, -3), (exp_e, -2), (norm1, 0), (ln_r, -2),
                     (ln_den, -2), (rstd2, -6), (evac_v, -1), (evac_h, 0), (exp_f2, -1),
                     ends=dict(rstd2=N // 2))

            def gate_tanhs(n):
                q = n % CPB
                bias = bias_t if n >= CPB else bias_0
                if n == 0:
                    act.wait_ge(S["bias_ready"], 3)
                act.wait_ge(S["gate_ps"], 3 * n + 1)
                after(act, "c_ready", n, CPB)
                a.activation(tf[:, q, :], G_PS[q][0][:, :], ACT.Tanh, scale=0.5,
                             bias=bias[:, 0:1]).then_inc(S["tf_ready"], 1)
                act.wait_ge(S["gate_ps"], 3 * n + 2)
                a.activation(ti[:, q, :], G_PS[q][1][:, :], ACT.Tanh, scale=0.5,
                             bias=bias[:, 1:2]).then_inc(S["ti_ready"], 1)
                act.wait_ge(S["gate_ps"], 3 * n + 3)
                a.activation(tg[:, q, :], G_PS[q][2][:, :], ACT.Tanh,
                             bias=bias[:, 2:3]).then_inc(S["tg_ready"], 1)

            def evac_uoc():
                act.wait_ge(S["uoc_ps"], 1)
                a.activation(uoc[:, :], UOC_PS[:, :], ACT.Identity, bias=col(BO)).then_inc(S["uoc_ready"], 1)

            def final_tanh(n):
                k = n % B
                if n < B:
                    after(act, "pre_ready", n)
                    a.activation(pre[:, k, :], pre[:, k, :], ACT.Tanh).then_inc(S["hf_ready"], 1)
                else:
                    after(act, "fin2_ps", n - B)
                    after(act, "ot_done", n, B)
                    a.activation(pre[:, k, :], FIN_PS[n][:, :], ACT.Tanh, bias=col(BO)).then_inc(S["hf_ready"], 1)

            evac_h2_hi(0)
            evac_h2(0)
            evac_h2_hi(1)
            rstd2(N // 2)
            evac_h2(1)
            a.preload_act_table_set("exp_and_others")
            gate_tanhs(0)
            evac_h2_hi(2)
            evac_h2(2)
            gate_tanhs(1)
            for n in range(CPB, N - 1):
                evac_h2_hi(n + 1)
                evac_h2(n + 1)
                gate_tanhs(n)
            gate_tanhs(N - 1)
            evac_uoc()
            for n in range(N):
                final_tanh(n)

        @block.vector
        def _(dve):
            v = nc.vector
            v.memset(eps_col[:], EPS).then_inc(S["eps_set"], 1)
            v.memset(w_full[:], 0.0).then_inc(S["eps_set"], 1)

            dve.wait_ge(S["silu_exp"], 1)
            v.tensor_scalar(silu_e[:], silu_e[:], 1.0, None, ALU.add).then_inc(S["silu_up"], 1)
            dve.wait_ge(S["silu_up"], 1)
            v.reciprocal(silu_e[:], silu_e[:]).then_inc(S["silu_up"], 1)
            dve.wait_ge(S["silu_up"], 2)
            v.tensor_tensor(silu[:], silu_e[:], cols[:, COND:COND + B], ALU.mult).then_inc(S["silu_ready"], 1)

            def weights_and_modulation():
                v.tensor_scalar(one_minus[:], cols[:, MIXK:MIXR + 1], -1.0, 1.0, ALU.mult,
                                ALU.add).then_inc(S["mix_ready"], 1)
                dve.wait_ge(S["decay_exp"], 1)
                v.tensor_scalar(w_col[:], w_col[:], -1.0, None, ALU.mult).then_inc(S["w_ready"], 1)
                dve.wait_ge(S["w_ready"], 1)
                dve.wait_ge(S["eps_set"], 2)
                v.tensor_scalar(w_full[:], w_full[:], w_col[:, 0:1], None, ALU.add).then_inc(S["w_ready"], 1)
                dve.wait_ge(S["ident_set"], 2)
                v.tensor_scalar(minus_ident[:], ident[:], -1.0, None, ALU.mult).then_inc(S["minus_ident_set"], 1)
                dve.wait_ge(S["mod_ps"], 1)
                v.tensor_copy(mods[:], MOD_PS[:, 0:6 * B]).then_inc(S["mods_sb"], 1)
                dve.wait_ge(S["mods_sb"], 1)
                scales = mods[:, :].rearrange("p (h s b) -> p h s b", h=2, s=3)[:, :, CA, :]
                v.tensor_scalar(scales, scales, 1.0, None, ALU.add).then_inc(S["mods_sb"], 1)
                dve.wait_ge(S["att_in"], 16)
                dve.wait_ge(S["mix_ready"], 1)
                for n in range(3):
                    v.tensor_scalar(w_now[:, n, :], w_att[:, WK + n, :], col(MIXK + n), None, ALU.mult)
                    v.tensor_scalar(w_prev[:, n, :], w_att[:, WK + n, :], one_minus[:, n:n + 1], None,
                                    ALU.mult).then_inc(S["kvr_w"], 1)

            def gated_wo():
                v.tensor_scalar(neg_g[:], mods[:], -1.0, None, ALU.mult).then_inc(S["neg_ready"], 1)
                v.tensor_scalar(sign_g[:], mods[:], 0.0, 2.0, ALU.is_ge, ALU.mult).then_inc(S["neg_ready"], 1)
                dve.wait_ge(S["neg_ready"], 2)
                v.scalar_tensor_tensor(out=neg_g[:], in0=neg_g[:], scalar=GATE_MIN, in1=mods[:], op0=ALU.max,
                                       op1=ALU.max).then_inc(S["neg_ready"], 1)
                dve.wait_ge(S["neg_ready"], 3)
                v.scalar_tensor_tensor(out=gates[:], in0=sign_g[:], scalar=-1.0, in1=neg_g[:], op0=ALU.add,
                                       op1=ALU.mult).then_inc(S["gates_ready"], 1)
                dve.wait_ge(S["gates_ready"], 1)
                for b in range(B):
                    last = v.tensor_scalar(wo_g[:, b, :], w_att[:, WO_ATT, :], gate(GA, b), None, ALU.mult)
                last.then_inc(S["wog_ready"], 1)

            def first_state():
                dve.wait_ge(S["wogT_ps"], 1)
                v.tensor_copy(wo_gT[:], WOG_PS[:, :]).then_inc(S["wogT_ready"], 1)
                dve.wait_ge(S["ffn_in"], 16)
                v.tensor_scalar(c2_0[:], col(INC), 2.0, None, ALU.mult).then_inc(S["c2_0_ready"], 1)
                v.tensor_scalar(bias_t[:, 0:2], cols[:, BF:BI + 1], 0.5, None, ALU.mult)
                v.tensor_copy(bias_t[:, 2:3], col(BC)).then_inc(S["bias_ready"], 1)

            def first_biases():
                dve.wait_ge(S["u_bias_ps"], 1)
                dve.wait_ge(S["bias_ready"], 1)
                v.scalar_tensor_tensor(out=bias_0[:, 0:2], in0=MOD_PS[:, 0:2], scalar=0.5, in1=bias_t[:, 0:2],
                                       op0=ALU.mult, op1=ALU.add).then_inc(S["bias_ready"], 1)
                v.tensor_tensor(bias_0[:, 2:3], MOD_PS[:, 2:3], bias_t[:, 2:3], ALU.add).then_inc(S["bias_ready"], 1)

            def split(weights, scale):
                v.tensor_scalar(w_hi[:, weights, :], w_ffn[:, weights, :], scale, None,
                                ALU.mult).then_inc(S["w_hi_ready"], 1)
                dve.wait_ge(S["w_hi_ready"], 1 if scale == 1.0 else 2)
                v.scalar_tensor_tensor(out=w_lo[:, weights, :], in0=w_ffn[:, weights, :], scalar=scale,
                                       in1=w_hi[:, weights, :].bitcast(F32), op0=ALU.mult,
                                       op1=ALU.subtract).then_inc(S["w_lo_ready"], 1)

            def split_w():
                split(slice(WF, UF), 1.0)

            def split_u():
                split(slice(UF, UO_FFN + 1), 0.5)

            later_setup = {1: gated_wo, 2: first_state, 3: first_biases, 4: split_w, 5: split_u}

            def token_stats(c, st, mv, part, ready):
                for j in range(J):
                    last = v.bn_stats(st[:, c, j, :], xs[:, c, j * C:(j + 1) * C])
                last.then_inc(S[part], 1)
                after(dve, part, c)
                for j in range(J):
                    last = v.bn_aggr(mv[:, c, j, :], st[:, c, j, :])
                last.then_inc(S[ready], 1)

            def stats1(c):
                dve.wait_ge(x_in[c], 16)
                token_stats(c, st1, mv1, "stats1a", "stats1_ready")

            def minus_mean1(c):
                after(dve, "rstd1_ready", c)
                v.scalar_tensor_tensor(out=nr1[:, c, :], in0=mv1[:, c, :, 0], scalar=-1.0, in1=rs1[:, c, :],
                                       op0=ALU.mult, op1=ALU.mult).then_inc(S["nr1_ready"], 1)
                if c < SHARED:
                    after(dve, "nr1_ready", c)
                    for j in range(J // 2, J):
                        last = v.tensor_scalar(xn1[:, c, j * C:(j + 1) * C], xs[:, c, j * C:(j + 1) * C],
                                               rs1[:, c, j:j + 1], nr1[:, c, j:j + 1], ALU.mult, ALU.add)
                    last.then_inc(S["xn1_half"], 1)
                if c == 0:
                    weights_and_modulation()

            def run_max(c):
                k, (m, o) = c % 2, at(c)
                if c in later_setup:
                    later_setup[c]()
                after(dve, "k_done", c)
                if c == 0:
                    dve.wait_ge(S["w_ready"], 2)
                    dve.wait_ge(S["edges_set"], 6)
                after(dve, "p_ready", c, 1)
                after(dve, "d1_ready", c, 2 * CPB)
                after(dve, "minus_p_done", c, 2 * CPB)
                if c % CPB == 0:
                    v.tensor_copy(pp[:, m, 0:1], K_PS[k][:, 0:1]).then_inc(S["p_start"], 1)
                    dve.wait_ge(S["p_start"], c // CPB + 1)
                v.tensor_tensor_scan(pp[:, m, o + 1:o + 1 + NT], w_full[:], K_PS[k][:, :], pp[:, m, o:o + 1],
                                     ALU.add, ALU.max).then_inc(S["p_ready"], 1)

            def d2(c):
                k, (m, o) = c % RING, at(c)
                after(dve, "p_ready", c)
                after(dve, "f2v_ready", c, RING)
                v.tensor_tensor(f2[:, k, :], K_PS[c % 2][:, :], pp[:, m, o + 1:o + 1 + NT],
                                ALU.subtract).then_inc(S["d2_ready"], 1)

            def cap_r(c):
                k = c % RING
                after(dve, "er_ready", c)
                v.tensor_scalar(er[:, k, :], er[:, k, :], CAP, None, ALU.min).then_inc(S["erc_ready"], 1)

            def scan_b(c):
                k, (m, o) = c % RING, at(c)
                after(dve, "f1_ready", c)
                after(dve, "f2_ready", c)
                after(dve, "b_ready", c, 1)
                v.tensor_tensor_scan(bb[:, m, o + 1:o + 1 + NT], f1[:, k, :], f2[:, k, :], bb[:, m, o:o + 1],
                                     ALU.mult, ALU.add).then_inc(S["b_ready"], 1)

            def scan_a(c):
                k, (m, o) = c % RING, at(c)
                after(dve, "f1_ready", c)
                after(dve, "f2v_ready", c)
                after(dve, "a_ready", c, 1)
                after(dve, "num_ready", c, 2 * CPB)
                v.tensor_tensor_scan(aa[:, m, o + 1:o + 1 + NT], f1[:, k, :], f2v[:, k, :], aa[:, m, o:o + 1],
                                     ALU.mult, ALU.add).then_inc(S["a_ready"], 1)

            def weigh_v(c):
                k = c % RING
                after(dve, "e_ready", c)
                after(dve, "v_ready", c)
                after(dve, "wo_done", c, RING)
                v.scalar_tensor_tensor(out=num[:, k, :], in0=ev[:, k, :], scalar=CAP, in1=vs[:, k, :],
                                       op0=ALU.min, op1=ALU.mult).then_inc(S["wv_ready"], 1)

            def den_(c):
                k, (m, o) = c % RING, at(c)
                after(dve, "e_ready", c)
                after(dve, "b_ready", c)
                after(dve, "y_ready", c, RING)
                v.scalar_tensor_tensor(out=den[:, k, :], in0=ev[:, k, :], scalar=CAP, in1=bb[:, m, o:o + NT],
                                       op0=ALU.min, op1=ALU.add).then_inc(S["den_ready"], 1)

            def residual(c):
                after(dve, "wo_done", c)
                v.tensor_tensor(xs[:, c, :], WO_PS[:, :], xs[:, c, :], ALU.add).then_inc(S["x2_ready"], 1)

            def stats2(c):
                after(dve, "x2_ready", c)
                token_stats(c, st2, mv2, "stats2a", "stats2_ready")

            def last_logs():
                k = (N - 1) % RING
                after(dve, "lr_ready", N - 1)
                after(dve, "ld_ready", N - 1)
                v.tensor_tensor(den[:, k, :], den[:, k, :], er[:, k, :], ALU.add).then_inc(S["last_logs"], 1)

            def last_num():
                k, (m, o) = (N - 1) % RING, at(N - 1)
                after(dve, "wv_ready", N - 1)
                after(dve, "a_ready", N - 1)
                v.tensor_tensor(num[:, k, :], num[:, k, :], aa[:, m, o:o + NT], ALU.add).then_inc(S["last_num"], 1)

            def last_y():
                k = (N - 1) % RING
                dve.wait_ge(S["last_num"], 1)
                after(dve, "rg_ready", N - 1)
                v.tensor_tensor(num[:, k, :], num[:, k, :], den[:, k, :], ALU.mult).then_inc(S["last_y"], 1)

            pipeline((stats1, 0), (scan_a, -3), (stats2, -5), (minus_mean1, 0), (scan_b, -2), (cap_r, -2), (run_max,
                     -1), (den_, -2), (residual, -4), (d2, -1), (weigh_v, -2),
                     ends=dict(scan_a=N - 1, scan_b=N - 1, cap_r=N - 1, den_=N - 1, weigh_v=N - 1, residual=5, stats2=4))
            scan_b(N - 1)
            cap_r(N - 1)
            residual(N - 3)
            den_(N - 1)
            weigh_v(N - 1)
            last_logs()
            scan_a(N - 1)
            last_num()
            last_y()
            residual(N - 2)


            def late_rstd2():
                half = slice(N // 2 + 1, N)
                after(dve, "stats2_ready", N - 1)
                v.tensor_scalar(nm2[:, half, :], mv2[:, half, :, 0], -1.0, None, ALU.mult)
                v.tensor_scalar(var_l[:], mv2[:, half, :, 1], EPS, None, ALU.add).then_inc(S["newton"], 1)
                dve.wait_ge(S["newton"], 1)
                v.tensor_scalar(bits_l[:], var_l[:].bitcast(I32), 1, None,
                                ALU.logical_shift_right).then_inc(S["newton"], 1)
                dve.wait_ge(S["newton"], 2)
                v.tensor_scalar(guess_l[:].bitcast(I32), bits_l[:], -1, 0x5F3759DF, ALU.mult,
                                ALU.add).then_inc(S["newton"], 1)
                for step in range(NEWTON):
                    dve.wait_ge(S["newton"], 3 + 3 * step)
                    v.tensor_tensor(y2_l[:], guess_l[:], guess_l[:], ALU.mult).then_inc(S["newton"], 1)
                    dve.wait_ge(S["newton"], 4 + 3 * step)
                    v.scalar_tensor_tensor(out=y2_l[:], in0=y2_l[:], scalar=-0.5, in1=var_l[:], op0=ALU.mult,
                                           op1=ALU.mult).then_inc(S["newton"], 1)
                    dve.wait_ge(S["newton"], 5 + 3 * step)
                    last = step == NEWTON - 1
                    v.scalar_tensor_tensor(out=rs2[:, half, :] if last else guess_l[:], in0=y2_l[:], scalar=1.5,
                                           in1=guess_l[:], op0=ALU.add,
                                           op1=ALU.mult).then_inc(S["rstd2_late" if last else "newton"], 1)

            def state(n):
                q = n % CPB
                after(dve, "tf_ready", n)
                if n >= CPB:
                    after(dve, "c_ready", n, CPB)
                    v.scalar_tensor_tensor(out=tf[:, q, :], in0=tf[:, q, :], scalar=1.0, in1=c2[:, q, :],
                                           op0=ALU.add, op1=ALU.mult).then_inc(S["fc_ready"], 1)
                else:
                    dve.wait_ge(S["c2_0_ready"], 1)
                    v.tensor_scalar(tf[:, q, :], tf[:, q, :], 1.0, c2_0[:, 0:1], ALU.add,
                                    ALU.mult).then_inc(S["fc_ready"], 1)
                after(dve, "ti_ready", n)
                after(dve, "tg_ready", n)
                v.scalar_tensor_tensor(out=ti[:, q, :], in0=ti[:, q, :], scalar=1.0, in1=tg[:, q, :],
                                       op0=ALU.add, op1=ALU.mult).then_inc(S["ig_ready"], 1)
                after(dve, "fc_ready", n)
                after(dve, "ig_ready", n)
                v.scalar_tensor_tensor(out=c2[:, q, :], in0=tf[:, q, :], scalar=0.5, in1=ti[:, q, :],
                                       op0=ALU.mult, op1=ALU.add).then_inc(S["c_ready"], 1)
                after(dve, "c_ready", n)
                v.tensor_copy(c2_hi[:, q, :], c2[:, q, :]).then_inc(S["c_hi_ready"], 1)
                after(dve, "c_hi_ready", n)
                v.tensor_tensor(c2_lo[:, q, :], c2[:, q, :], c2_hi[:, q, :].bitcast(F32),
                                ALU.subtract).then_inc(S["c_lo_ready"], 1)

            def before_tanh(n):
                k = n % B
                after(dve, "fin_ps", n)
                dve.wait_ge(S["uoc_ready"], 1)
                v.tensor_tensor(pre[:, k, :], FIN_PS[n][:, :], uoc[:, :], ALU.add).then_inc(S["pre_ready"], 1)

            def output(n):
                q, t = FINALS[n]
                c = t * CPB + q
                after(dve, "ot_done", n)
                v.tensor_tensor(xs[:, c, :], OT_PS[n % 2][:, :], xs[:, c, :], ALU.add).then_inc(S["out_ready"], 1)

            stats2(N - 4)
            stats2(N - 3)
            stats2(N - 2)
            residual(N - 1)
            stats2(N - 1)
            state(0)
            state(1)
            late_rstd2()
            state(2)
            state(3)
            state(N - 4)
            state(N - 3)
            state(N - 2)
            state(N - 1)
            for n in range(B):
                before_tanh(n)
            for n in range(N):
                output(n)

        @block.tensor
        def _(pe):
            t_ = nc.tensor
            pe.wait_ge(S["ident_set"], 2)
            for _ in range(WARM_UP):
                t_.matmul(MOD_PS[:, 0:P], ident[:, :], ident[:, :], start=True, stop=True)
            pe.wait_ge(S["mod_in"], 16)
            pe.wait_ge(S["silu_ready"], 1)
            for s in range(6):
                last = t_.matmul(MOD_PS[:, s * B:(s + 1) * B], w_att[:, WMOD + s, :], silu[:], start=True, stop=True)
            last.then_inc(S["mod_ps"], 1)
            for _ in range(0):
                t_.matmul(V_PS[:, 0:P], ident[:, :], ident[:, :], start=True, stop=True)

            def turn1(c):
                k = c % RING
                after(pe, "xn1_ready", c)
                if c < SHARED:
                    after(pe, "xn1_half", c)
                after(pe, "h_ready", c, 1)
                if c == 0:
                    pe.wait_ge(S["ident_set"], 2)
                for j in range(J):
                    last = t_.transpose(T1_PS[:, j * P:(j + 1) * P], xn1[:, k, j * C:(j + 1) * C], ident[:, :])
                last.then_inc(S["t1_done"], 1)
                if c == 0:
                    for _ in range(4):
                        t_.matmul(V_PS[:, 0:P], ident[:, :], ident[:, :], start=True, stop=True)

            def project(c, n, bank, done):
                m, o = at(c)
                after(pe, "h_ready", c)
                if c == 0:
                    pe.wait_ge(S["kvr_w"], n + 1)
                    pe.wait_ge(S["edges_set"], 6)
                t_.matmul(bank[:, :], w_now[:, n, :], hh[:, m, o + 1:o + 1 + NT], start=True, stop=False)
                t_.matmul(bank[:, :], w_prev[:, n, :], hh[:, m, o:o + NT], start=False,
                          stop=True).then_inc(S[done], 1)

            def project_k(c):
                after(pe, "e_ready", c, 2)
                project(c, 0, K_PS[c % 2], "k_done")

            def project_v(c):
                after(pe, "v_ready", c, 1)
                project(c, 1, V_PS, "v_done")

            def project_r(c):
                after(pe, "er_ready", c, 1)
                project(c, 2, R_PS, "r_done")

            def minus_p(c):
                m, o = at(c)
                after(pe, "d2_ready", c)
                if c == 0:
                    pe.wait_ge(S["minus_ident_set"], 1)
                t_.matmul(K_PS[c % 2][:, :], minus_ident[:, :], pp[:, m, o:o + NT], start=False, stop=True,
                          skip_group_check=True).then_inc(S["minus_p_done"], 1)
                if c == 1:
                    pe.wait_ge(S["wog_ready"], 1)
                    for b in range(B):
                        last = t_.transpose(WOG_PS[:, b * C:(b + 1) * C], wo_g[:, b, :], ident[:, :])
                    last.then_inc(S["wogT_ps"], 1)
                if c == 2:
                    pe.wait_ge(S["ffn_in"], 16)
                    for n in range(3):
                        last = t_.matmul(MOD_PS[:, n:n + 1], w_ffn[:, UF + n, :], col(INC), start=True, stop=True)
                    last.then_inc(S["u_bias_ps"], 1)

            def turn2(c):
                after(pe, "xn2_ready", c)
                after(pe, "h2_ready", c, 2)
                if c == 0:
                    pe.wait_ge(S["bias_ready"], 3)
                for j in range(J):
                    last = t_.transpose(T2_PS[c % 2][:, j * P:(j + 1) * P], xn2[:, c % 2, j * C:(j + 1) * C],
                                        ident[:, :])
                last.then_inc(S["t2_done"], 1)

            def keep_clock(products):
                pe.wait_ge(S["h_ready"], N)
                for _ in range(products):
                    t_.matmul(T1_PS[:, 0:P], ident[:, :], ident[:, :], start=True, stop=True)

            def project_out(c):
                k = c % RING
                if c < N - 1:
                    after(pe, "y_ready", c)
                else:
                    pe.wait_ge(S["last_y"], 1)
                if c == 0:
                    pe.wait_ge(S["wogT_ready"], 1)
                after(pe, "x2_ready", c, 1)
                y = num[:, k, :].rearrange("q (p j) -> q j p", j=J)
                b = c // CPB
                for j in range(J):
                    last = t_.matmul(WO_PS[:, j * C:(j + 1) * C], y[:, j, :], wo_gT[:, b * C:(b + 1) * C],
                                     start=True, stop=True)
                last.then_inc(S["wo_done"], 1)

            pipeline((project_out, -4), (project_v, -1), (turn1, 0), (project_r, -1), (minus_p, -1), (project_k, 0),
                     ends=dict(project_out=N - 2))

            def by_high(bank, weights, x_hi, start, stop=False):
                t_.matmul(bank[:, :], w_hi[:, weights, :], x_hi, start=start, stop=False)
                return t_.matmul(bank[:, :], w_lo[:, weights, :], x_hi, start=False, stop=stop)

            def by_low(bank, weights, x_lo, stop):
                return t_.matmul(bank[:, :], w_hi[:, weights, :], x_lo, start=False, stop=stop)

            def gates_x(n):
                q = n % CPB
                after(pe, "h2_hi_ready", n)
                if n == 0:
                    pe.wait_ge(S["w_lo_ready"], 2)
                    pe.wait_ge(S["e_ready"], N)
                    pe.wait_ge(S["v_ready"], N)
                if n == 1:
                    pe.wait_ge(S["er_ready"], N)
                for w, read in enumerate(("tf_ready", "ti_ready", "tg_ready")):
                    after(pe, read, n, CPB)
                    if n == CPB - 1 and w == 2:
                        after(pe, "x2_ready", N - 1)
                    by_high(G_PS[q][w], WF + w, h2_hi[:, n, :], start=True)
                if CPB <= n + 1 < N:
                    turn2(n + 1)
                after(pe, "h2_lo_ready", n)
                for w in range(3):
                    last = by_low(G_PS[q][w], WF + w, h2_lo[:, n, :], stop=(n < CPB))
                    if n < CPB:
                        last.then_inc(S["gate_ps"], 1)

            def gates_c(n):
                q = n % CPB
                after(pe, "c_hi_ready", n, CPB)
                for w in range(3):
                    by_high(G_PS[q][w], UF + w, c2_hi[:, q, :], start=False)
                after(pe, "c_lo_ready", n, CPB)
                for w in range(3):
                    by_low(G_PS[q][w], UF + w, c2_lo[:, q, :], stop=True).then_inc(S["gate_ps"], 1)

            def final_c():
                after(pe, "c_hi_ready", N - 2)
                by_high(UOC_PS, UO_FFN, c2_hi[:, 0, :], start=True)
                after(pe, "c_lo_ready", N - 2)
                by_low(UOC_PS, UO_FFN, c2_lo[:, 0, :], stop=True).then_inc(S["uoc_ps"], 1)

            def final_x(n):
                q, t = FINALS[n]
                c = t * CPB + q
                if B <= n < B + 3:
                    after(pe, ("tf_ready", "ti_ready", "tg_ready")[n - B], N - 1)
                elif n >= B + 3:
                    pe.wait_ge(S["uoc_ready"], 1)
                elif n >= 2:
                    pe.wait_ge(S["h2_ready"], N)
                    pe.wait_ge(S["h2_hi_ready"], N)
                by_high(FIN_PS[n], WO_FFN, h2_hi[:, c, :], start=True)
                last = by_low(FIN_PS[n], WO_FFN, h2_lo[:, c, :], stop=(n < B))
                if n < B:
                    last.then_inc(S["fin_ps"], 1)

            def final_xc(n):
                after(pe, "c_hi_ready", N - 1)
                by_high(FIN_PS[n], UO_FFN, c2_hi[:, 1, :], start=False)
                after(pe, "c_lo_ready", N - 1)
                by_low(FIN_PS[n], UO_FFN, c2_lo[:, 1, :], stop=True).then_inc(S["fin2_ps"], 1)

            def turn_back(n):
                k = n % B
                after(pe, "hg_ready", n)
                after(pe, "out_ready", n, 2)
                if n < 2:
                    after(pe, "pre_ready", n + 2)
                for j in range(J):
                    last = t_.transpose(OT_PS[n % 2][:, j * C:(j + 1) * C], pre[:, k, j * P:(j + 1) * P], ident[:, :])
                last.then_inc(S["ot_done"], 1)

            keep_clock(4)
            project_out(N - 2)
            keep_clock(8)
            turn2(0)
            turn2(1)
            project_out(N - 1)
            keep_clock(4)
            gates_x(0)
            for n in range(1, N):
                gates_x(n)
                if n >= CPB:
                    gates_c(n)
            final_c()
            final_x(0)
            final_x(1)
            final_x(2)
            final_x(3)
            final_x(4)
            final_x(5)
            final_x(6)
            final_x(7)
            final_xc(4)
            turn_back(0)
            final_xc(5)
            turn_back(1)
            turn_back(2)
            final_xc(6)
            turn_back(3)
            final_xc(7)
            turn_back(4)
            turn_back(5)
            turn_back(6)
            turn_back(7)


def kernel(**inputs):
    import numpy as _np
    import concourse.bacc as _bacc
    from concourse import mybir as _mybir
    from concourse.bass_utils import run_bass_kernel_spmd as _run

    a = {name: _np.asarray(v) for name, v in inputs.items()}
    x = _np.ascontiguousarray(a["L0_attn_x"])
    columns = [a[f"L0_attn_{n}"].reshape(-1) for n in ("time_decay", "time_first", "time_mix_k", "time_mix_v",
                                                       "time_mix_r")]
    columns += [a[f"L0_ffn_{n}"] for n in ("bf", "bi", "bc", "bo", "in_c")]
    arrays = {
        "x": x,
        "small": _np.stack([*columns, *a["L0_c"]], axis=1),
        "att_w": _np.concatenate([a["L0_attn_Wk"].T, a["L0_attn_Wv"].T, a["L0_attn_Wr"].T, a["L0_attn_Wo"],
                                  a["L0_wmod"]], axis=1),
        "ffn_w": _np.concatenate([a[f"L0_ffn_{n}"].T for n in ("wf", "wi", "wc", "wo", "uf", "ui", "uc", "uo")],
                                 axis=1),
    }
    nc = _bacc.Bacc("TRN2", target_bir_lowering=False, num_devices=1)
    args = [nc.dram_tensor(n, v.shape, _mybir.dt.from_np(v.dtype), kind="ExternalInput").ap()
            for n, v in arrays.items()]
    args.append(nc.dram_tensor("out_0", x.shape, F32, kind="ExternalOutput").ap())
    adaln_rwkv_block_kernel(nc, *args)
    r = _run(nc, [arrays], core_ids=[0])
    return r.results[0]["out_0"]
```
